# Optimizing a Trainium2 kernel written in Bass

```python
import numpy as np
import jax
import jax.numpy as jnp

def _softmax(x, axis=-1):
    return jax.nn.softmax(x, axis=axis)

def _gelu(x):
    return jax.nn.gelu(x, approximate=True)

def _silu(x):
    return jax.nn.silu(x)

def _sigmoid(x):
    return jax.nn.sigmoid(x)

def _layernorm(x, axis=-1, eps=1e-05):
    m = jnp.mean(x, axis=axis, keepdims=True)
    v = jnp.var(x, axis=axis, keepdims=True)
    return (x - m) / jnp.sqrt(v + eps)

def _scatter_add(tgt, idx, src, axis=0):
    return tgt.at[idx].add(src)

def _segment_sum(src, seg, n):
    return jax.ops.segment_sum(src, seg, n)
kernel_name = 'mk_cond_resid_d4_seqx_r4_1ca3c1'

def setup_inputs(seed: int=0):
    np.random.seed(seed)
    _w = jnp.asarray

    def _rec_inputs():
        import jax
        import jax.numpy as jnp
        _rk = jax.random.key(seed)
        x = -7.109e-05 + 0.9999 * jax.random.normal(jax.random.fold_in(_rk, 1), (32, 64, 1024), jnp.float32)
        _lenS = 64 - jax.random.randint(jax.random.fold_in(_rk, 7), (32,), 0, max(1, 64 // 4) + 1, jnp.int32)
        _lenS2 = 64 - jax.random.randint(jax.random.fold_in(_rk, 8), (32,), 0, max(1, 64 // 4) + 1, jnp.int32)
        itok_B_0_15 = jax.random.randint(jax.random.fold_in(_rk, 11), (32,), 0, 16, jnp.int32)
        itok_B_2_6 = jax.random.randint(jax.random.fold_in(_rk, 12), (32,), 2, 7, jnp.int32)
        itok_B_78_3631 = jax.random.randint(jax.random.fold_in(_rk, 13), (32,), 78, 908, jnp.int32)
        itok_B_0_31 = jax.random.randint(jax.random.fold_in(_rk, 14), (32,), 0, 32, jnp.int32)
        return (x, itok_B_0_15, itok_B_2_6, itok_B_78_3631, itok_B_0_31)
    x, itok_B_0_15, itok_B_2_6, itok_B_78_3631, itok_B_0_31 = _rec_inputs()

    def _L0_cond_setup():
        import jax, jax.numpy as jnp
        import numpy as np
        NUM_CONDITIONS = 16
        IN_CH = 64
        OUT_CH = 64
        B = 64
        T = 1024
        key = jax.random.key(seed)
        k_x, k_w, k_c = jax.random.split(key, 3)
        x = jax.random.normal(k_x, (B, IN_CH, T), dtype=jnp.float32)
        bound = float(np.sqrt(6.0 / IN_CH))
        weights = jax.random.uniform(k_w, (NUM_CONDITIONS, IN_CH, OUT_CH), dtype=jnp.float32, minval=-bound, maxval=bound)
        condition = jax.random.randint(k_c, (B,), 0, NUM_CONDITIONS, dtype=jnp.int64)
        return {'x': x, 'weights': weights, 'condition': condition}
    _L0_cond_all = _L0_cond_setup()
    _L0_cond_in = {k: v for k, v in _L0_cond_all.items() if k in ('weights',)}
    del _L0_cond_all

    def _L1_cond_setup():
        import jax, jax.numpy as jnp
        import numpy as np
        B, N, H, F = (4, 128, 1024, 2752)
        L, R, RANK = (1, 16, 16)
        SCALE = 0.5
        key = jax.random.key(seed)
        ks = jax.random.split(key, 12)
        nrm = lambda k, shape, fan: jax.random.normal(k, shape, jnp.float32) * fan ** (-0.5)
        inp = {'x': jax.random.normal(ks[0], (B, N, H), jnp.float32), 'W_gate': nrm(ks[1], (F, H), H), 'W_up': nrm(ks[2], (F, H), H), 'W_down': nrm(ks[3], (H, F), F), 'A_gate': nrm(ks[4], (L, R, RANK, H), H), 'B_gate': nrm(ks[5], (L, R, F, RANK), RANK), 'A_up': nrm(ks[6], (L, R, RANK, H), H), 'B_up': nrm(ks[7], (L, R, F, RANK), RANK), 'A_down': nrm(ks[8], (L, R, RANK, F), F), 'B_down': nrm(ks[9], (L, R, H, RANK), RANK), 'lora_indices': jax.random.randint(ks[10], (B,), 0, R), 'layer_idx': 0}
        return inp
    _L1_cond_all = _L1_cond_setup()
    _L1_cond_in = {k: v for k, v in _L1_cond_all.items() if k in ('W_gate', 'W_up', 'W_down', 'A_gate', 'B_gate', 'A_up', 'B_up', 'A_down', 'B_down')}
    del _L1_cond_all

    def _L2_cond_setup():
        import math
        import jax, jax.numpy as jnp
        import numpy as np
        B, H, N, L = (16, 64, 64, 1024)
        DT_MIN, DT_MAX = (0.001, 0.1)

        def _get_kernel(log_dt, C, log_A_real, A_imag, length):
            dt = jnp.exp(log_dt)
            Cc = C[..., 0] + 1j * C[..., 1]
            A = -jnp.exp(log_A_real) + 1j * A_imag
            dtA = A * dt[:, None]
            Ct = Cc * (jnp.exp(dtA) - 1.0) / A
            P = dtA[:, :, None] * jnp.arange(length, dtype=jnp.float32)
            K = 2.0 * jnp.einsum('hn,hnl->hl', Ct, jnp.exp(P)).real
            return K
        key = jax.random.key(seed)
        ks = jax.random.split(key, 5)
        u = jax.random.normal(ks[0], (B, H, L), dtype=jnp.float32)
        log_dt = jax.random.uniform(ks[1], (H,), dtype=jnp.float32) * (math.log(DT_MAX) - math.log(DT_MIN)) + math.log(DT_MIN)
        C = jax.random.normal(ks[2], (H, N, 2), dtype=jnp.float32)
        log_A_real = jnp.log(0.5 * jnp.ones((H, N), dtype=jnp.float32))
        A_imag = math.pi * jnp.broadcast_to(jnp.arange(N, dtype=jnp.float32), (H, N))
        D = jax.random.normal(ks[3], (H,), dtype=jnp.float32)
        length = jax.random.randint(ks[4], (B,), 1, L + 1, dtype=jnp.int32)
        return {'u': u, 'log_dt': log_dt, 'C': C, 'log_A_real': log_A_real, 'A_imag': A_imag, 'D': D, 'length': length}
    _L2_cond_all = _L2_cond_setup()
    _L2_cond_in = {k: v for k, v in _L2_cond_all.items() if k in ('log_dt', 'C', 'log_A_real', 'A_imag', 'D')}
    del _L2_cond_all

    def _L3_cond_setup():
        import jax, jax.numpy as jnp
        import numpy as np
        S, C, D = (32, 64, 64)
        B, T = (64, 1024)
        key = jax.random.key(seed)
        k_x, k_w, k_s = jax.random.split(key, 3)
        x = jax.random.normal(k_x, (B, C, T), dtype=jnp.float32)
        subjects = jax.random.randint(k_s, (B,), 0, S, dtype=jnp.int64)
        std = float(np.sqrt(2.0 / (C + D)))
        weights = jax.random.normal(k_w, (S, C, D), dtype=jnp.float32) * std * (1.0 / np.sqrt(C))
        biases = jnp.zeros((S, 1, D), dtype=jnp.float32)
        return {'x': x, 'subjects': subjects, 'weights': weights, 'biases': biases}
    _L3_cond_all = _L3_cond_setup()
    _L3_cond_in = {k: v for k, v in _L3_cond_all.items() if k in ('weights', 'biases')}
    del _L3_cond_all
    return {'x': x, 'itok_B_0_15': itok_B_0_15, 'itok_B_2_6': itok_B_2_6, 'itok_B_78_3631': itok_B_78_3631, 'itok_B_0_31': itok_B_0_31, 'L0_cond_weights': _L0_cond_in['weights'], 'L1_cond_W_gate': _L1_cond_in['W_gate'], 'L1_cond_W_up': _L1_cond_in['W_up'], 'L1_cond_W_down': _L1_cond_in['W_down'], 'L1_cond_A_gate': _L1_cond_in['A_gate'], 'L1_cond_B_gate': _L1_cond_in['B_gate'], 'L1_cond_A_up': _L1_cond_in['A_up'], 'L1_cond_B_up': _L1_cond_in['B_up'], 'L1_cond_A_down': _L1_cond_in['A_down'], 'L1_cond_B_down': _L1_cond_in['B_down'], 'L2_cond_log_dt': _L2_cond_in['log_dt'], 'L2_cond_C': _L2_cond_in['C'], 'L2_cond_log_A_real': _L2_cond_in['log_A_real'], 'L2_cond_A_imag': _L2_cond_in['A_imag'], 'L2_cond_D': _L2_cond_in['D'], 'L3_cond_weights': _L3_cond_in['weights'], 'L3_cond_biases': _L3_cond_in['biases']}

def reference(x, itok_B_0_15, itok_B_2_6, itok_B_78_3631, itok_B_0_31, L0_cond_weights, L1_cond_W_gate, L1_cond_W_up, L1_cond_W_down, L1_cond_A_gate, L1_cond_B_gate, L1_cond_A_up, L1_cond_B_up, L1_cond_A_down, L1_cond_B_down, L2_cond_log_dt, L2_cond_C, L2_cond_log_A_real, L2_cond_A_imag, L2_cond_D, L3_cond_weights, L3_cond_biases):
    import jax
    import jax.numpy as jnp

    def _L0_cond_ref(x, weights, condition):
        import jax, jax.numpy as jnp
        import numpy as np
        NUM_CONDITIONS = 16
        IN_CH = 64
        OUT_CH = 64
        B = 64
        T = 1024
        W = weights[condition]
        return jnp.einsum('bct,bcd->bdt', x, W)

    def _L1_cond_ref(x, W_gate, W_up, W_down, A_gate, B_gate, A_up, B_up, A_down, B_down, lora_indices, layer_idx):
        import jax, jax.numpy as jnp
        import numpy as np
        B, N, H, F = (4, 128, 1024, 2752)
        L, R, RANK = (1, 16, 16)
        SCALE = 0.5

        def lora_add(base, inp, A, B):
            Ab = A[layer_idx][lora_indices]
            Bb = B[layer_idx][lora_indices]
            t = jnp.einsum('bri,bni->bnr', Ab, inp)
            return base + jnp.einsum('bor,bnr->bno', Bb, t) * SCALE
        gate = lora_add(jnp.einsum('bnh,fh->bnf', x, W_gate), x, A_gate, B_gate)
        up = lora_add(jnp.einsum('bnh,fh->bnf', x, W_up), x, A_up, B_up)
        act = jax.nn.silu(gate) * up
        down = lora_add(jnp.einsum('bnf,hf->bnh', act, W_down), act, A_down, B_down)
        return down

    def _L2_cond_ref(u, log_dt, C, log_A_real, A_imag, D, length):
        import math
        import jax, jax.numpy as jnp
        import numpy as np
        B, H, N, L = (16, 64, 64, 1024)
        DT_MIN, DT_MAX = (0.001, 0.1)

        def _get_kernel(log_dt, C, log_A_real, A_imag, length):
            dt = jnp.exp(log_dt)
            Cc = C[..., 0] + 1j * C[..., 1]
            A = -jnp.exp(log_A_real) + 1j * A_imag
            dtA = A * dt[:, None]
            Ct = Cc * (jnp.exp(dtA) - 1.0) / A
            P = dtA[:, :, None] * jnp.arange(length, dtype=jnp.float32)
            K = 2.0 * jnp.einsum('hn,hnl->hl', Ct, jnp.exp(P)).real
            return K
        Bq, Hq, Lq = u.shape
        K = _get_kernel(log_dt, C, log_A_real, A_imag, Lq)
        n = 2 * Lq
        kf = jnp.fft.rfft(K, n=n)
        uf = jnp.fft.rfft(u, n=n)
        y = jnp.fft.irfft(uf * kf[None], n=n)[..., :Lq]
        y = y + u * D[:, None]
        mask = (jnp.arange(Lq)[None, :] < length[:, None]).astype(u.dtype)
        return y * mask[:, None, :]

    def _L3_cond_ref(x, subjects, weights, biases):
        import jax, jax.numpy as jnp
        import numpy as np
        S, C, D = (32, 64, 64)
        B, T = (64, 1024)
        w = weights[subjects]
        b = biases[subjects]
        out = jnp.einsum('bct,bcd->bdt', x, w)
        return out + jnp.transpose(b, (0, 2, 1))
    x = x + _L0_cond_ref(x, L0_cond_weights, itok_B_0_15)
    x = x + _L1_cond_ref(x, L1_cond_W_gate, L1_cond_W_up, L1_cond_W_down, L1_cond_A_gate, L1_cond_B_gate, L1_cond_A_up, L1_cond_B_up, L1_cond_A_down, L1_cond_B_down, itok_B_2_6, 0)
    x = x + _L2_cond_ref(x, L2_cond_log_dt, L2_cond_C, L2_cond_log_A_real, L2_cond_A_imag, L2_cond_D, itok_B_78_3631)
    x = x + _L3_cond_ref(x, itok_B_0_31, L3_cond_weights, L3_cond_biases)
    return x

_drawn_inputs = setup_inputs


def setup_inputs(seed=0):
    import zlib

    import numpy as np

    out = dict(_drawn_inputs(seed))
    spreads = {'L2_cond_log_A_real': (-0.6931471824645996, 0.2), 'L3_cond_biases': (0.0, 0.493)}
    factors = {}
    for name, (base, spread) in spreads.items():
        noise = np.random.default_rng([zlib.crc32(name.encode()), seed]).standard_normal(out[name].shape)
        drawn = base * np.exp(spread * noise) if base else spread * noise
        out[name] = jnp.asarray(drawn.astype(out[name].dtype))
    for name, factor in factors.items():
        out[name] = (out[name] * factor).astype(out[name].dtype)
    return out
```

```python
from contextlib import ExitStack

import concourse.bass as bass
import numpy as np
from concourse import mybir

ALU = mybir.AluOpType
ACT = mybir.ActivationFunctionType
F32 = mybir.dt.float32
F32R = mybir.dt.float32r
I32 = mybir.dt.int32

P = 128
B, C, T = 32, 64, 1024
F, RANK = 2752, 16
NCOND, NLORA, NSUBJ = 16, 16, 32
NST = 64

NCH = 4
CB = B // NCH
TOK = CB * C
KB = T // P
PAIRS = B // 2
CP = CB // 2
FULL = F // P
REST = F - FULL * P
FB = FULL + 1
GU = 2 * FULL + 1
HALF = FB // 2
AD_UNITS = ((0, 8), (8, 15), (15, 22))
UNITS = 2 + GU + len(AD_UNITS) + 2 * KB
U_DOWN = 2 + GU + len(AD_UNITS)
US = UNITS // 2
assert REST * 2 == P and UNITS % 2 == 0 and U_DOWN % 2 == 0 and TOK == 512

LS = 32
KROW = T + P
TRING, URING = 4, 4
ROUND = 1.5 * 2.0 ** 23
LN2_HI, LN2_LO = 0.693359375, -2.12194440e-4
CONSTS_KERNEL, CONSTS = 6, 19
KG_TH, KG_EXP, KG_SIN = 17, 24, 42
KG_UV = 83
TWO_PI = 6.283185


def build(nc, x, cond, lora, length, subj, w0, wgu, wd, agu, ad, bgu, bd, log_dt, c_ri, log_ar, a_im,
          d_skip, w3, bias, out):
    ctx = ExitStack()
    with ctx:
        def sem(name):
            return ctx.enter_context(nc.semaphore(name))

        def dram(name, shape):
            return nc.dram_tensor(name, shape, F32).ap()

        agu_of = dram("agu_of_batches", (NCH, P, CB * 2 * KB * RANK))
        ad_of = dram("ad_of_batches", (NCH, P, CB, FB * RANK))
        bgu_of = dram("bgu_of_batches", (NCH, P, (GU + 1) * P))
        bd_of = dram("bd_of_batches", (NCH, P, T))
        x1_dram = dram("x1_dram", (NCH, P, KB, TOK))
        k_dram = dram("k_dram", (C, KROW))

        base = (nc.sbuf_base + 63) // 64 * 64

        def place(at, items):
            tiles = []
            for name, shape, dt in items:
                tiles.append(nc.alloc_sbuf_tensor_at(name, shape, dt, offset=at))
                at += (int(np.prod(shape[1:])) * 4 + 63) // 64 * 64
            assert at <= nc.sbuf_usable_end, (at, nc.sbuf_usable_end)
            return tiles, at

        (ids, ident, w0bd, mask4, mask8, len_i, len_f), at = place(base, [
            ("ids", [1, 4, B], I32), ("ident", [P, P], F32), ("w0bd", [P, PAIRS, P], F32),
            ("mask4", [P, CB // 2], F32), ("mask8", [P, CB], F32),
            ("len_i", [P, B], I32), ("len_f", [P, B], F32)])
        stage_base = at
        (xn, xhi, xlo, raw, whi, wlo, t_hi, t_lo, t32, silu, act32, x1out), at = place(stage_base, [
            ("xn", [P, CP, T], F32), ("xhi", [P, KB, TOK], F32R), ("xlo", [P, KB, TOK], F32R),
            ("raw", [P, 2, 12, P], F32), ("whi", [P, 2, 12, P], F32R), ("wlo", [P, 2, 12, P], F32R),
            ("t_hi", [P, 2, TOK], F32R), ("t_lo", [P, 2, TOK], F32R), ("t32", [P, TOK], F32),
            ("silu", [P, TOK], F32), ("act32", [P, TOK], F32), ("x1out", [P, 2, TOK], F32)])
        act_base = at
        (act_hi, act_lo), at = place(act_base, [
            ("act_hi", [P, FB, TOK], F32R), ("act_lo", [P, FB, TOK], F32R)])
        small = "aim cre cim adt w1 w2 adt32 wc tmp th s1 c1 sh em er ei n2 qr qi cr ci al be".split()
        sm, at = place(act_base, [("s4_" + n, [P, C], F32) for n in small])
        s = dict(zip(small, sm))
        (ex_x, ex_k, ex_r, ex_p, ex_t, ex_i), at = place(at, [
            (n, [P, 2, C], I32 if n == "ex_i" else F32) for n in "ex_x ex_k ex_r ex_p ex_t ex_i".split()])
        s |= {"dt_": ex_x[:, 0, :], "ea": ex_x[:, 1, :]}
        (jj, ph, drow, last, dexp, vv, ve, uu, ue, ux, rr, ksb, kzero), _ = place(at, [
            ("jj", [P, LS], F32), ("ph", [P, 1], F32), ("drow", [1, C], F32),
            ("last", [1, LS], F32), ("dexp", [1, C, LS], F32),
            ("vv", [P, C, LS], F32), ("ve", [P, C, LS], F32), ("uu", [P, C, LS], F32),
            ("ue", [P, C, LS], F32), ("ux", [P, C, LS], F32), ("rr", [P, C, LS], F32),
            ("ksb", [LS, C, LS], F32), ("kzero", [C, P], F32)])
        (rtoep, toep, mask, yv, ug, bcol, w3bd, x2n, ostage, x1s), _ = place(stage_base, [
            ("rtoep", [P, TRING, T], F32), ("toep", [P, TRING, T], F32), ("mask", [P, KB, B], F32), ("yv", [P, 2, KB, B], F32),
            ("ug", [P, URING, KB, B], F32), ("bcol", [P, PAIRS], F32), ("w3bd", [P, PAIRS, P], F32),
            ("x2n", [P, 2, T], F32), ("ostage", [P, 2, T], F32), ("x1s", [P, NCH, KB, TOK], F32)])

        ps = ctx.enter_context(nc.psum_tensor("ps", [P, 8, 512], F32))
        GATE, UP, DOWN, TDB, L0B = 0, 1, 2, 6, 4

        ids_in = sem("ids_in")
        par_in = sem("par_in")
        consts = sem("consts")
        w0_in = sem("w0_in")
        w0_ready = sem("w0_ready")
        gathered = sem("gathered")
        kg = sem("kernel_step")
        k_stored = sem("k_stored")
        x_in = [sem(f"x_in{q}") for q in range(CP)]
        l0_done = sem("l0_done")
        l0_hi = sem("l0_hi")
        l0_lo = sem("l0_lo")
        raw_in = [sem(f"raw_in{i}") for i in range(2)]
        hi_done = [sem(f"hi_done{i}") for i in range(2)]
        lo_done = [sem(f"lo_done{i}") for i in range(2)]
        unit_done = [sem(f"unit_done{i}") for i in range(2)]
        t_step = sem("t_step")
        t_ready = sem("t_ready")
        silu_done = sem("silu_done")
        mul_done = sem("mul_done")
        act_hi_done = sem("act_hi_done")
        act_done = sem("act_done")
        res_step = sem("res_step")
        x1_ready = sem("x1_ready")
        x1_stored = [sem(f"x1_stored{i}") for i in range(2)]
        conv_init = sem("conv_init")
        mask_ready = sem("mask_ready")
        w3_in = sem("w3_in")
        w3_ready = sem("w3_ready")
        x1_in = sem("x1_in")
        toep_in = [sem(f"toep_in{i}") for i in range(TRING)]
        ug_ready = sem("ug_ready")
        toep_ready = sem("toep_ready")
        conv_done = sem("conv_done")
        y_done = sem("y_done")
        x2_done = sem("x2_done")
        turned = sem("turned")
        x2n_ready = sem("x2n_ready")
        l3_done = sem("l3_done")
        out_ready = sem("out_ready")
        out_stored = [sem(f"out_stored{i}") for i in range(2)]
        CREDIT_CONV, CREDIT_Y, CREDIT_X1 = TRING, 2, 2

        block = ctx.enter_context(nc.Block())

        def nth(c, u):
            return c * US + (u // 2 + 1)

        xr = x.rearrange("(c q p) t -> c p q t", c=NCH, q=CP)
        outr = out.rearrange("(n p) t -> n p t", p=P)

        def split_views(u):
            i = u % 2
            if u < 2:
                r = raw[:, i, 0:KB, :].rearrange("p a b -> p (a b)").rearrange(
                    "p (b g k r) -> p g b k r", b=CB // 2, g=2, r=RANK)
                return [(r[:, g], lambda t, g=g: t[:, i, 0:KB, :].rearrange(
                    "p k (g b r) -> p g b k r", g=2, r=RANK)[:, g]) for g in range(2)]
            if U_DOWN > u >= 2 + GU:
                k0, k1 = AD_UNITS[u - 2 - GU]
                n = k1 - k0
                r = raw[:, i, 0:n, :].rearrange("p a b -> p (a b)").rearrange(
                    "p (b k r) -> p b k r", b=CB, r=RANK)
                return [(r, lambda t: t[:, i, 0:n, :].rearrange("p k (b r) -> p b k r", r=RANK))]
            n = KB + 2 if u == 1 + GU else KB + 1 if u < U_DOWN else HALF + u % 2
            return [(raw[:, i, 0:n, :], lambda t: t[:, i, 0:n, :])]

        @block.sync
        def _(sp):
            def load_x(c):
                for q in range(CP):
                    if not (isinstance(c, int) and c == 0):
                        sp.wait_ge(l0_done, (c - 1) * CP + q + 1)
                    sp.dma_start(xn[:, q, :], xr[c, :, q, :]).then_inc(x_in[q], 16)

            def load_unit(c, u, parts):
                i = u % 2
                sp.wait_ge(lo_done[i], nth(c, u))
                for dst, src in parts:
                    sp.dma_start(dst, src).then_inc(raw_in[i], 16)

            def flat(i, a, b):
                return raw[:, i, :, :].rearrange("p a b -> p (a b)")[:, a:b]

            def chunk(c, last):
                sp.wait_ge(gathered, (c * CB + CB) * 16 * 4)
                n = CB // 2 * 2 * KB * RANK
                for u in range(2):
                    load_unit(c, u, [(flat(u, g * n // 2, (g + 1) * n // 2),
                                      agu_of[c, :, u * n + g * n // 2:u * n + (g + 1) * n // 2])
                                     for g in range(2)])

                with sp.Fori(0, FULL) as f:
                    for g in range(2):
                        sp.wait_ge(lo_done[g], nth(c, 2) + f)
                        sp.dma_start(raw[:, g, 0:KB, :], wgu[2 * f + g]).then_inc(raw_in[g], 16)
                        sp.dma_start(raw[:, g, KB, :],
                                     bgu_of[c, :, bass.ds((2 * f + g) * P, P)]).then_inc(raw_in[g], 16)
                u = 2 + GU - 1
                load_unit(c, u, [(raw[:, 0, 0:KB, :], wgu[GU - 1]),
                                 (flat(0, KB * P, (KB + 2) * P), bgu_of[c, :, (GU - 1) * P:(GU + 1) * P])])
                for n, (k0, k1) in enumerate(AD_UNITS):
                    u = 2 + GU + n
                    w = (k1 - k0) * RANK
                    dst = flat(u % 2, 0, CB * w).rearrange("p (b w) -> p b w", w=w)
                    load_unit(c, u, [(dst[:, b:b + CB // 2, :],
                                      ad_of[c, :, b:b + CB // 2, k0 * RANK:k1 * RANK])
                                     for b in (0, CB // 2)])
                if not last:
                    load_x(c + 1)
                with sp.Fori(0, KB) as lb:
                    for i in range(2):
                        sp.wait_ge(lo_done[i], nth(c, U_DOWN) + lb)
                        if i == 0:
                            sp.dma_start(raw[:, 0, 0:6, :], wd[lb, 0, :, 0:6, :]).then_inc(raw_in[0], 16)
                            sp.dma_start(raw[:, 0, 6:HALF, :], wd[lb, 0, :, 6:HALF, :]).then_inc(raw_in[0], 16)
                        else:
                            sp.dma_start(raw[:, 1, 0:HALF, :], wd[lb, 1]).then_inc(raw_in[1], 16)
                            sp.dma_start(raw[:, 1, HALF, :],
                                         bd_of[c, :, bass.ds(lb * P, P)]).then_inc(raw_in[1], 16)

            load_x(0)
            with sp.Fori(0, NCH - 1) as c:
                chunk(c, False)
            chunk(NCH - 1, True)

            sp.wait_ge(unit_done[1], NCH * US + 1)
            for i in range(2):
                sp.wait_ge(x1_stored[i], 16 + 16 * NCH * KB // 2)
            for c in range(NCH):
                sp.dma_start(x1s[:, c, :, :], x1_dram[c]).then_inc(x1_in, 16)
            sp.wait_ge(k_stored, 32)
            kt = bass.AP(k_dram.tensor, 0, [[KROW, C], [1, P], [1, T]])
            with sp.Fori(0, C // TRING) as g:
                for j in range(TRING):
                    sp.wait_ge(toep_ready, g * TRING + (j + 1))
                    sp.dma_start(rtoep[:, j, :], kt[g * TRING + j]).then_inc(toep_in[j], 16)
            for n in range(PAIRS):
                sp.wait_ge(out_ready, n + 1)
                sp.dma_start(outr[n], ostage[:, n % 2, :]).then_inc(out_stored[n % 2], 16)
            for i in range(2):
                sp.wait_ge(out_stored[i], 16 * PAIRS // 2)

        @block.gpsimd
        def _(pool):
            pool.dma_start(ids[0:1, 0, :], cond).then_inc(ids_in, 16)
            pool.dma_start(ids[0:1, 1, :], lora).then_inc(ids_in, 16)
            pool.dma_start(ids[0:1, 2, :], subj).then_inc(ids_in, 16)
            made = [0]

            def const(ins):
                ins.then_inc(consts, 1)
                made[0] += 1
                pool.wait_ge(consts, made[0])

            def select(tile, op, fill, base, pattern, m):
                const(pool.affine_select(out=tile, in_=tile, compare_op=op, fill=fill, base=base,
                                         pattern=pattern, channel_multiplier=m))
            const(pool.iota(jj[:, :], pattern=[[-1, LS]], base=LS - 1, channel_multiplier=0,
                            allow_small_or_imprecise_dtypes=True))
            const(pool.memset(ph[0:C, :], 0.25))
            const(pool.memset(ph[C:P, :], 0.0))
            const(pool.memset(last[:, :], 0.0))
            const(pool.memset(last[0:1, LS - 1:LS], 1.0))
            const(pool.memset(dexp[:, :, :], 0.0))
            assert made[0] == CONSTS_KERNEL
            const(pool.memset(ident[:, :], 0.0))
            select(ident[:, :], ALU.not_equal, 1.0, 0, [[-1, P]], 1)
            halves = [(mask4[64 * g:64 * g + 64, :], CB // 2) for g in range(2)]
            for m, n in [(mask8[:, :], CB)] + halves:
                const(pool.memset(m, 0.5))
                select(m, ALU.is_ge, 0.0, 0, [[-RANK, n]], 1)
                select(m, ALU.is_ge, 0.0, RANK - 1, [[RANK, n]], -1)
            const(pool.memset(kzero[:, :], 0.0))
            const(pool.memset(w0bd[:, :, :], 0.0))
            assert made[0] == CONSTS
            pool.wait_ge(ids_in, 48)
            w0v = w0bd[:, :, :].rearrange("p n (g d) -> p n g d", g=2)
            with pool.Fori(0, PAIRS) as n:
                for g in range(2):
                    k = pool.value_load(ids[0:1, 0, bass.ds(2 * n + g, 1)], min_val=0, max_val=NCOND - 1)
                    pool.dma_start(w0v[64 * g:64 * g + 64, bass.ds(n, 1), g, :],
                                   w0[bass.ds(k, 1)].rearrange("o c d -> c o d")).then_inc(w0_in, 16)
            with pool.Fori(0, NCH) as c:
                with pool.Fori(0, CB) as b:
                    k = pool.value_load(ids[0:1, 1, bass.ds(c * CB + b, 1)], min_val=0, max_val=NLORA - 1)
                    wa = 2 * KB * RANK
                    pool.dma_start(agu_of[c, :, bass.ds(b * wa, wa)], agu[k]).then_inc(gathered, 16)
                    pool.dma_start(bgu_of[c, bass.ds(b * RANK, RANK), :], bgu[k]).then_inc(gathered, 16)
                    pool.dma_start(ad_of[c, :, b, :], ad[k]).then_inc(gathered, 16)
                    pool.dma_start(bd_of[c, bass.ds(b * RANK, RANK), :], bd[k]).then_inc(gathered, 16)
                pool.wait_ge(gathered, (c * CB + CB) * 16 * 4)
            pool.wait_ge(unit_done[1], NCH * US + 1)
            for i in range(2):
                pool.wait_ge(x1_stored[i], 16 + 16 * NCH * KB // 2)
            pool.memset(w3bd[:, :, :], 0.0).then_inc(conv_init, 1)
            pool.iota(mask[:, :, :], pattern=[[P, KB], [0, B]], base=0, channel_multiplier=1,
                      allow_small_or_imprecise_dtypes=True).then_inc(mask_ready, 1)
            pool.wait_ge(conv_init, 1)
            w3v = w3bd[:, :, :].rearrange("p n (g d) -> p n g d", g=2)
            with pool.Fori(0, PAIRS) as n:
                for g in range(2):
                    k = pool.value_load(ids[0:1, 2, bass.ds(2 * n + g, 1)], min_val=0, max_val=NSUBJ - 1)
                    pool.dma_start(w3v[64 * g:64 * g + 64, bass.ds(n, 1), g, :],
                                   w3[bass.ds(k, 1)].rearrange("o c d -> c o d")).then_inc(w3_in, 16)
                    pool.dma_start(bcol[64 * g:64 * g + 64, bass.ds(n, 1)],
                                   bias[bass.ds(k, 1), :].rearrange("o d -> d o")).then_inc(w3_in, 16)
            pool.wait_ge(x1_in, 16 * NCH)
            x1h = x1s[:, :, :, :].rearrange("p c l (b h) -> p l c b h", h=C)
            with pool.Fori(0, C // URING) as g:
                for j in range(URING):
                    pool.wait_ge(conv_done, g * URING + (j + 1 - URING + CREDIT_CONV))
                    pool.tensor_copy(ug[:, j, :, :].rearrange("p l (c b) -> p l c b", c=NCH),
                                     x1h[:, :, :, :, g * URING + j]).then_inc(ug_ready, 1)

        @block.scalar
        def _(act):
            def load(dst, src):
                act.dma_start(dst, src).then_inc(par_in, 16)
            load(ex_x[:, 0, :], log_dt.partition_broadcast(P))
            load(drow[0:1, :], d_skip)
            load(len_i[:, :], length.partition_broadcast(P))
            for g in range(2):
                rows = slice(64 * g, 64 * g + 64)
                load(ex_x[rows, 1, :], log_ar)
                load(s["aim"][rows, :], a_im)
                load(s["cre"][rows, :], c_ri[0])
                load(s["cim"][rows, :], c_ri[1])
            act.wait_ge(par_in, 11 * 16)

            def fn(dst, src, f, scale=1.0):
                act.activation(dst, src, f, scale=scale).then_inc(kg, 1)
            act.wait_ge(kg, KG_TH)
            fn(s["th"][:, :], s["adt"][:, :], ACT.Tanh, 0.5)
            act.wait_ge(kg, KG_EXP)
            fn(ve[:, :, :], ve[:, :, :], ACT.Exp)
            fn(ue[:, :, :], ue[:, :, :], ACT.Exp)
            act.wait_ge(kg, KG_SIN)
            fn(s["s1"][:, :], s["w1"][:, :], ACT.Sin, TWO_PI)
            fn(s["c1"][:, :], s["wc"][:, :], ACT.Sin, TWO_PI)
            fn(s["sh"][:, :], s["w1"][:, :], ACT.Sin, TWO_PI / 2)
            fn(vv[:, :, :], vv[:, :, :], ACT.Sin, TWO_PI)
            fn(uu[:, :, :], uu[:, :, :], ACT.Sin, TWO_PI)
            fn(ux[:, :, :], ux[:, :, :], ACT.Sin, TWO_PI)

            act.wait_ge(kg, KG_UV + 2)
            act.dma_start(k_dram[:, T:KROW], kzero[:, :]).then_inc(k_stored, 16)
            act.dma_start(k_dram[:, 0:T].rearrange("h (a j) -> a h j", j=LS), ksb[:, :, :]).then_inc(k_stored, 16)

            def hi(c, u):
                i = u % 2
                n = nth(c, u)
                act.wait_ge(raw_in[i], n * 32)
                act.wait_ge(unit_done[i], n)
                for r, w in split_views(u):
                    ins = act.activation(w(whi), r, ACT.Copy)
                ins.then_inc(hi_done[i], 1)

            with act.Fori(0, NCH) as c:
                hi(c, 0)
                hi(c, 1)
                act.wait_ge(x1_ready, c * KB + CREDIT_X1)
                for q in range(CP):
                    act.wait_ge(l0_done, c * CP + q + 1)
                    b = L0B + 2 * (q % 2)
                    act.activation(xhi[:, :, q * P:(q + 1) * P],
                                   ps[:, b:b + 2, :].rearrange("p b (k m) -> p (b k) m", m=P),
                                   ACT.Copy).then_inc(l0_hi, 1)
                with act.Fori(0, FULL) as f:
                    for g in range(2):
                        act.wait_ge(raw_in[g], (nth(c, 2) + f) * 32)
                        act.wait_ge(unit_done[g], nth(c, 2) + f)
                        act.activation(whi[:, g, 0:KB + 1, :], raw[:, g, 0:KB + 1, :],
                                       ACT.Copy).then_inc(hi_done[g], 1)
                    act.wait_ge(unit_done[0], nth(c, 2) + f + 1)
                    act.wait_ge(mul_done, c * FB + f + 1)
                    act.activation(silu[:, :], ps[:, GATE, :], ACT.Silu).then_inc(silu_done, 1)
                u = 2 + GU - 1
                hi(c, u)
                hi(c, u + 1)
                act.wait_ge(unit_done[0], nth(c, u) + 1)
                act.wait_ge(mul_done, c * FB + FULL + 1)
                act.activation(silu[0:REST, :], ps[0:REST, GATE, :], ACT.Silu).then_inc(silu_done, 1)
                hi(c, u + 2)
                hi(c, u + 3)

                def store(lb, par):
                    act.wait_ge(x1_ready, c * KB + lb + (1 + CREDIT_X1))
                    act.dma_start(x1_dram[c, :, lb, :], x1out[:, par, :]).then_inc(x1_stored[par], 16)

                hi(c, U_DOWN)
                hi(c, U_DOWN + 1)
                with act.Fori(0, KB // 2 - 1) as h:
                    for par in range(2):
                        for i in range(2):
                            n = nth(c, U_DOWN) + h * 2 + (par + 1)
                            act.wait_ge(raw_in[i], n * 32)
                            act.wait_ge(unit_done[i], n)
                            act.activation(whi[:, i, 0:HALF + i, :], raw[:, i, 0:HALF + i, :],
                                           ACT.Copy).then_inc(hi_done[i], 1)
                        store(h * 2 + par, par)
                hi(c, UNITS - 2)
                hi(c, UNITS - 1)
                store(KB - 2, 0)
                store(KB - 1, 1)

            with act.Fori(0, C // TRING) as g:
                for j in range(TRING):
                    act.wait_ge(toep_in[j], g * 16 + 16)
                    act.wait_ge(conv_done, g * TRING + (j + 1))
                    act.activation(toep[:, j, :], rtoep[:, j, ::-1], ACT.Copy).then_inc(toep_ready, 1)

            for n in range(PAIRS):
                act.wait_ge(turned, n + 1)
                if n >= 2:
                    act.wait_ge(l3_done, n - 1)
                b = 2 * (n % 2)
                act.activation(x2n[:, n % 2, :], ps[:, b:b + 2, :].rearrange("p a t -> p (a t)"),
                               ACT.Copy).then_inc(x2n_ready, 1)

        @block.tensor
        def _(pe):
            def products(bank, w, nblk, r_hi, r_lo, start, stop, first=0):
                for k in range(first, first + nblk):
                    for n, (wt, r) in enumerate(((whi, r_hi), (whi, r_lo), (wlo, r_hi))):
                        ins = pe.matmul(bank, wt[:, w, k, :], r(k), start=start and k == first and n == 0,
                                        stop=stop and k == first + nblk - 1 and n == 2)
                return ins

            pe.wait_ge(kg, KG_UV)
            per_bank = 512 // LS
            for h in range(C):
                hb = h % per_bank
                if hb == 0:
                    pe.matmul(ps[0:LS, h // per_bank, :], last[:, :],
                              dexp[:, h:h + per_bank, :].rearrange("p h j -> p (h j)"), start=True, stop=False)
                ins = pe.matmul(ps[0:LS, h // per_bank, hb * LS:(hb + 1) * LS], uu[:, h, :], vv[:, h, :],
                                start=False, stop=hb == per_bank - 1)
            ins.then_inc(kg, 1)

            pe.wait_ge(w0_ready, 1)
            with pe.Fori(0, NCH) as c:
                pe.wait_ge(x1_ready, c * KB + CREDIT_X1)
                for q in range(CP):
                    pe.wait_ge(x_in[q], c * 16 + 16)
                    if q >= 2:
                        pe.wait_ge(l0_lo, c * CP + q - 1)
                    b = L0B + 2 * (q % 2)
                    for k in range(KB):
                        ins = pe.matmul(ps[:, b + k // 4, (k % 4) * P:(k % 4) * P + P],
                                        xn[:, q, k * P:(k + 1) * P],
                                        w0bd[:, bass.ds(c * CP + q, 1), :].rearrange("p o d -> p (o d)"),
                                        start=True, stop=True)
                    ins.then_inc(l0_done, 1)
                for u in range(2):
                    pe.wait_ge(l0_lo, c * CP + 2 * u + 2)
                    pe.wait_ge(lo_done[u], nth(c, u) + 1)
                    t0 = u * TOK // 2
                    products(ps[:, DOWN + u, 0:TOK // 2], u, KB, lambda k: xhi[:, k, t0:t0 + TOK // 2],
                             lambda k: xlo[:, k, t0:t0 + TOK // 2], True, True).then_inc(unit_done[u], 1)

                def x_hi(k):
                    return xhi[:, k, :]

                def x_lo(k):
                    return xlo[:, k, :]

                def lora_b(bank, w, k, g, cols=slice(0, P)):
                    for n, (wt, t) in enumerate(((whi, t_hi), (whi, t_lo), (wlo, t_hi))):
                        ins = pe.matmul(bank, wt[:, w, k, cols], t[:, g, :], start=False, stop=n == 2)
                    return ins

                with pe.Fori(0, FULL) as f:
                    pe.wait_ge(silu_done, c * FB + f + 1)
                    pe.wait_ge(lo_done[0], nth(c, 2) + f + 1)
                    products(ps[:, GATE, :], 0, KB, x_hi, x_lo, True, False)
                    pe.wait_ge(t_ready, c * 5 + 5)
                    lora_b(ps[:, GATE, :], 0, KB, 0).then_inc(unit_done[0], 1)
                    pe.wait_ge(mul_done, c * FB + f + 1)
                    pe.wait_ge(lo_done[1], nth(c, 2) + f + 1)
                    products(ps[:, UP, :], 1, KB, x_hi, x_lo, True, False)
                    lora_b(ps[:, UP, :], 1, KB, 1).then_inc(unit_done[1], 1)
                u = 2 + GU - 1
                pe.wait_ge(silu_done, c * FB + FULL + 1)
                pe.wait_ge(lo_done[0], nth(c, u) + 1)
                products(ps[:, GATE, :], 0, KB, x_hi, x_lo, True, False)
                lora_rest = ((whi, t_hi), (whi, t_lo), (wlo, t_hi))
                for n, (wt, t) in enumerate(lora_rest):
                    pe.matmul(ps[:, GATE, :], wt[:, 0, KB, :], t[:, 0, :], start=False, stop=False)
                for n, (wt, t) in enumerate(lora_rest):
                    ins = pe.matmul(ps[:, GATE, :], wt[:, 0, KB + 1, :], t[:, 1, :], start=False, stop=n == 2)
                ins.then_inc(unit_done[0], 1)
                for n, (k0, k1) in enumerate(AD_UNITS):
                    u = 2 + GU + n
                    pe.wait_ge(act_done, c * FB + k1 + 1)
                    pe.wait_ge(lo_done[u % 2], nth(c, u) + 1)
                    products(ps[:, TDB, :], u % 2, k1 - k0, lambda k: act_hi[:, k0 + k, :],
                             lambda k: act_lo[:, k0 + k, :], n == 0,
                             n == len(AD_UNITS) - 1).then_inc(unit_done[u % 2], 1)
                with pe.Fori(0, KB // 2) as h:
                    for par in range(2):
                        bank = ps[:, DOWN + par, :]
                        n = nth(c, U_DOWN) + h * 2 + par
                        pe.wait_ge(x1_ready, c * KB + h * 2 + (par + CREDIT_X1 - 1))
                        pe.wait_ge(lo_done[0], n + 1)
                        products(bank, 0, HALF, lambda k: act_hi[:, k, :], lambda k: act_lo[:, k, :],
                                 True, False).then_inc(unit_done[0], 1)
                        pe.wait_ge(lo_done[1], n + 1)
                        products(bank, 1, HALF, lambda k: act_hi[:, HALF + k, :],
                                 lambda k: act_lo[:, HALF + k, :], False, False)
                        pe.wait_ge(t_ready, c * 5 + 6)
                        lora_b(bank, 1, HALF, 0).then_inc(unit_done[1], 1)

            with pe.Fori(0, C // TRING) as g:
                for j in range(TRING):
                    h = g * TRING + j
                    pe.wait_ge(toep_ready, h + (1 + TRING))
                    pe.wait_ge(ug_ready, h + 1)
                    pe.wait_ge(y_done, h + (1 + CREDIT_Y - 2))
                    y = ps[:, j % 2, 0:KB * B]
                    u = ug[:, j % URING, :, :].rearrange("p l b -> p (l b)")
                    for d in range(KB):
                        ins = pe.matmul(y[:, d * B:], toep[:, j, d * P:(d + 1) * P], u[:, 0:(KB - d) * B],
                                        start=d == 0, stop=d == KB - 1)
                    ins.then_inc(conv_done, 1)

            pe.wait_ge(x2_done, C + CREDIT_Y)
            pe.wait_ge(w3_ready, 1)

            def turn(n):
                if n >= 2:
                    pe.wait_ge(x2n_ready, n - 1)
                for k in range(KB):
                    ins = pe.transpose(ps[:, 2 * (n % 2) + k // 4, (k % 4) * P:(k % 4) * P + P],
                                       x1s[:, n // CP, k, (n % CP) * P:(n % CP) * P + P], ident[:, :])
                ins.then_inc(turned, 1)

            turn(0)
            for n in range(PAIRS):
                if n + 1 < PAIRS:
                    turn(n + 1)
                pe.wait_ge(x2n_ready, n + 1)
                if n >= 2:
                    pe.wait_ge(out_ready, n - 1)
                for k in range(2):
                    ins = pe.matmul(ps[:, 4 + 2 * (n % 2) + k, :], w3bd[:, n, :],
                                    x2n[:, n % 2, k * 512:(k + 1) * 512], start=True, stop=True)
                ins.then_inc(l3_done, 1)

        @block.vector
        def _(dve):
            for i in range(2):
                dve.sem_inc(lo_done[i], 1)
                dve.sem_inc(unit_done[i], 1)
                dve.sem_inc(x1_stored[i], 16)
            dve.sem_inc(silu_done, 1)
            dve.sem_inc(mul_done, 1)
            dve.sem_inc(act_done, 1)
            dve.sem_inc(t_ready, 1)
            dve.sem_inc(x2_done, CREDIT_Y)
            dve.sem_inc(x1_ready, CREDIT_X1)
            dve.sem_inc(conv_done, CREDIT_CONV)
            dve.sem_inc(toep_ready, TRING)
            dve.sem_inc(y_done, CREDIT_Y)

            step = [0]

            def did(ins):
                ins.then_inc(kg, 1)
                step[0] += 1

            def after(n=None):
                dve.wait_ge(kg, step[0] if n is None else n)

            def per_h(t):
                return t[:, :].unsqueeze(2).to_broadcast([P, C, LS])

            powers = jj[:, :].unsqueeze(1).to_broadcast([P, C, LS])
            tt, ts, stt = dve.tensor_tensor, dve.tensor_scalar, dve.scalar_tensor_tensor

            def a(n):
                return s[n][:, :]

            dve.wait_ge(consts, CONSTS_KERNEL)
            dve.wait_ge(par_in, 11 * 16)
            dve.tensor_copy(len_f[:, :], len_i[:, :]).then_inc(t_step, 1)
            did(dve.tensor_copy(dexp[:, :, LS - 1], drow[:, :]))
            xe, ke, re_, pe_, te = (t[:, :, :] for t in (ex_x, ex_k, ex_r, ex_p, ex_t))
            did(ts(ke, xe, float(1 / np.log(2)), None, ALU.mult))
            after()
            did(ts(te, ke, ROUND, -ROUND, ALU.add, ALU.add))
            after()
            did(ts(ke, te, -126.0, 127.0, ALU.max, ALU.min))
            after()
            did(stt(re_, ke, -LN2_HI, xe, ALU.mult, ALU.add))
            after()
            did(stt(re_, ke, -LN2_LO, re_, ALU.mult, ALU.add))
            did(ts(te, ke, 127.0, 2.0 ** 23, ALU.add, ALU.mult))
            after()
            did(dve.tensor_copy(ex_i[:, :, :], te))
            did(ts(pe_, re_, 1 / 5040, None, ALU.mult))
            for k in (720, 120, 24, 6, 2, 1):
                after()
                did(stt(pe_, pe_, 1 / k, re_, ALU.add, ALU.mult))
            after()
            did(stt(ex_x[:, :, :], pe_, 1.0, ex_i[:, :, :].bitcast(F32), ALU.add, ALU.mult))
            after()
            did(stt(a("adt"), a("ea"), -1.0, a("dt_"), ALU.mult, ALU.mult))
            assert step[0] == KG_TH, step
            after()
            step[0] += 1
            did(ts(a("adt32"), a("adt"), float(LS), None, ALU.mult))
            did(tt(ve[:, :, :], per_h(s["adt"]), powers, ALU.mult))
            did(stt(a("w1"), a("aim"), 1 / (2 * np.pi), a("dt_"), ALU.mult, ALU.mult))
            after()
            did(tt(ue[:, :, :], per_h(s["adt32"]), powers, ALU.mult))
            did(ts(a("tmp"), a("w1"), ROUND, -ROUND, ALU.add, ALU.add))
            after()
            did(tt(a("w1"), a("w1"), a("tmp"), ALU.subtract))
            assert step[0] == KG_EXP, step
            after()
            step[0] += 2
            did(ts(a("w2"), a("w1"), float(LS), None, ALU.mult))
            did(ts(a("wc"), a("w1"), 0.25, None, ALU.add))
            did(tt(vv[:, :, :], per_h(s["w1"]), powers, ALU.mult))
            after()
            did(ts(a("tmp"), a("w2"), ROUND, -ROUND, ALU.add, ALU.add))
            did(ts(a("em"), a("wc"), ROUND, -ROUND, ALU.add, ALU.add))
            did(ts(vv[:, :, :], vv[:, :, :], ph[:, 0:1], None, ALU.add))
            after()
            did(tt(a("w2"), a("w2"), a("tmp"), ALU.subtract))
            did(tt(a("wc"), a("wc"), a("em"), ALU.subtract))
            did(ts(rr[:, :, :], vv[:, :, :], ROUND, -ROUND, ALU.add, ALU.add))
            after()
            did(tt(uu[:, :, :], per_h(s["w2"]), powers, ALU.mult))
            did(tt(vv[:, :, :], vv[:, :, :], rr[:, :, :], ALU.subtract))
            after()
            did(ts(ux[:, :, :], uu[:, :, :], 0.25, None, ALU.add))
            did(ts(rr[:, :, :], uu[:, :, :], ROUND, -ROUND, ALU.add, ALU.add))
            after()
            did(tt(uu[:, :, :], uu[:, :, :], rr[:, :, :], ALU.subtract))
            after()
            did(ts(rr[:, :, :], ux[:, :, :], ROUND, -ROUND, ALU.add, ALU.add))
            after()
            did(tt(ux[:, :, :], ux[:, :, :], rr[:, :, :], ALU.subtract))
            assert step[0] == KG_SIN, step
            step[0] += 6
            after()
            did(ts(a("tmp"), a("th"), -1.0, 1.0, ALU.mult, ALU.add))
            did(tt(a("sh"), a("sh"), a("sh"), ALU.mult))
            did(tt(a("n2"), a("ea"), a("ea"), ALU.mult))
            did(tt(a("cr"), a("aim"), a("aim"), ALU.mult))
            after()
            did(dve.reciprocal(a("tmp"), a("tmp")))
            did(tt(a("n2"), a("n2"), a("cr"), ALU.add))
            after()
            did(stt(a("em"), a("th"), 2.0, a("tmp"), ALU.mult, ALU.mult))
            did(dve.reciprocal(a("n2"), a("n2")))
            after()
            did(tt(a("er"), a("em"), a("c1"), ALU.mult))
            did(stt(a("ei"), a("em"), 1.0, a("s1"), ALU.add, ALU.mult))
            after()
            did(stt(a("er"), a("sh"), -2.0, a("er"), ALU.mult, ALU.add))
            after()
            did(tt(a("qr"), a("ei"), a("aim"), ALU.mult))
            did(tt(a("tmp"), a("er"), a("ea"), ALU.mult))
            did(tt(a("qi"), a("ei"), a("ea"), ALU.mult))
            did(tt(a("cr"), a("er"), a("aim"), ALU.mult))
            after()
            did(tt(a("qr"), a("qr"), a("tmp"), ALU.subtract))
            did(tt(a("qi"), a("qi"), a("cr"), ALU.add))
            after()
            did(tt(a("qr"), a("qr"), a("n2"), ALU.mult))
            did(stt(a("qi"), a("qi"), -1.0, a("n2"), ALU.mult, ALU.mult))
            after()
            did(tt(a("cr"), a("cre"), a("qr"), ALU.mult))
            did(tt(a("tmp"), a("cim"), a("qi"), ALU.mult))
            did(tt(a("ci"), a("cre"), a("qi"), ALU.mult))
            did(tt(a("er"), a("cim"), a("qr"), ALU.mult))
            after()
            did(tt(a("cr"), a("cr"), a("tmp"), ALU.subtract))
            did(tt(a("ci"), a("ci"), a("er"), ALU.add))
            after()
            did(ts(s["al"][0:C, :], s["cr"][0:C, :], 2.0, None, ALU.mult))
            did(ts(s["al"][C:P, :], s["ci"][C:P, :], -2.0, None, ALU.mult))
            did(ts(s["be"][0:C, :], s["ci"][0:C, :], -2.0, None, ALU.mult))
            did(ts(s["be"][C:P, :], s["cr"][C:P, :], -2.0, None, ALU.mult))
            did(tt(vv[:, :, :], vv[:, :, :], ve[:, :, :], ALU.mult))
            did(tt(uu[:, :, :], uu[:, :, :], ue[:, :, :], ALU.mult))
            did(tt(ux[:, :, :], ux[:, :, :], ue[:, :, :], ALU.mult))
            after()
            did(tt(uu[:, :, :], uu[:, :, :], per_h(s["be"]), ALU.mult))
            did(tt(ux[:, :, :], ux[:, :, :], per_h(s["al"]), ALU.mult))
            after()
            did(tt(uu[:, :, :], uu[:, :, :], ux[:, :, :], ALU.add))
            assert step[0] == KG_UV, step
            dve.wait_ge(consts, CONSTS)
            dve.wait_ge(w0_in, 16 * B)
            tt(w0bd[:, :, :], w0bd[:, :, :], ident[:, :].unsqueeze(1).to_broadcast([P, PAIRS, P]),
               ALU.add).then_inc(w0_ready, 1)
            dve.memset(t_hi[:, :, :].bitcast(F32), 0.0).then_inc(t_step, 1)
            dve.memset(t_lo[:, :, :].bitcast(F32), 0.0).then_inc(t_step, 1)
            step[0] += 1
            after()
            did(dve.tensor_copy(ksb[:, :, :].rearrange("p h j -> p (h j)"),
                                ps[0:LS, 0:4, :].rearrange("p a b -> p (a b)")))
            dve.wait_ge(k_stored, 32)
            dve.memset(act_hi[REST:P, FB - 1, :].bitcast(F32), 0.0).then_inc(t_step, 1)
            dve.memset(act_lo[REST:P, FB - 1, :].bitcast(F32), 0.0).then_inc(t_step, 1)
            dve.wait_ge(t_step, 5)

            def f32(t):
                return t.bitcast(F32)

            def lo(c, u):
                i = u % 2
                dve.wait_ge(hi_done[i], nth(c, u))
                for r, w in split_views(u):
                    ins = tt(w(wlo), r, f32(w(whi)), ALU.subtract)
                ins.then_inc(lo_done[i], 1)

            TS0 = 5
            TSC = 10

            def lora_t(c, piece, src, rows, cols, g, m, bats):
                n = TS0 + 2 * piece
                base_ = c * TSC
                dve.wait_ge(t_ready, c * 5 + (piece + 1))
                dst = t32[rows, cols].rearrange("p (b n) -> p b n", b=bats)
                tt(dst, src.rearrange("p (b n) -> p b n", b=bats),
                   m.unsqueeze(2).to_broadcast([src.shape[0], bats, C]), ALU.mult).then_inc(t_step, 1)
                dve.wait_ge(t_step, base_ + n + 1)
                dve.tensor_copy(t_hi[rows, g, cols], t32[rows, cols]).then_inc(t_step, 1)
                dve.wait_ge(t_step, base_ + n + 2)
                tt(t_lo[rows, g, cols], t32[rows, cols], f32(t_hi[rows, g, cols]),
                   ALU.subtract).then_inc(t_ready, 1)

            def gate_up(c, f, rows, up):
                n = c * FB + f
                dve.wait_ge(silu_done, n + 2)
                dve.wait_ge(act_done, n + 1)
                tt(act32[rows, :], silu[rows, :], up, ALU.mult).then_inc(mul_done, 1)
                dve.wait_ge(mul_done, n + 2)
                a_hi = act_hi[rows, bass.ds(f, 1), :].rearrange("p o t -> p (o t)")
                a_lo = act_lo[rows, bass.ds(f, 1), :].rearrange("p o t -> p (o t)")
                dve.tensor_copy(a_hi, act32[rows, :]).then_inc(act_hi_done, 1)
                dve.wait_ge(act_hi_done, n + 1)
                tt(a_lo, act32[rows, :], f32(a_hi), ALU.subtract).then_inc(act_done, 1)

            def residual(c, lb, par, free):
                dve.wait_ge(unit_done[1], nth(c, U_DOWN + 1) + lb + 1)
                dve.wait_ge(x1_stored[par], free)
                o = x1out[:, par, :]
                tt(o, ps[:, DOWN + par, :], f32(xhi[:, bass.ds(lb, 1), :]).rearrange("p o t -> p (o t)"),
                   ALU.add).then_inc(res_step, 1)
                dve.wait_ge(res_step, c * KB + lb + 1)
                tt(o, o, f32(xlo[:, bass.ds(lb, 1), :]).rearrange("p o t -> p (o t)"),
                   ALU.add).then_inc(x1_ready, 1)

            full = slice(0, P)
            with dve.Fori(0, NCH) as c:
                lo(c, 0)
                lo(c, 1)
                for q in range(CP):
                    dve.wait_ge(l0_hi, c * CP + q + 1)
                    b = L0B + 2 * (q % 2)
                    sl = slice(q * P, (q + 1) * P)
                    tt(xlo[:, :, sl], ps[:, b:b + 2, :].rearrange("p b (k m) -> p (b k) m", m=P),
                       f32(xhi[:, :, sl]), ALU.subtract).then_inc(l0_lo, 1)
                lo(c, 2)
                piece = 0
                for u in range(2):
                    dve.wait_ge(unit_done[u], nth(c, u) + 1)
                    for g in range(2):
                        rows = slice(64 * u, 64 * u + 64)
                        cols = slice(u * TOK // 2, (u + 1) * TOK // 2)
                        lora_t(c, piece, ps[64 * g:64 * g + 64, DOWN + u, 0:TOK // 2], rows, cols, g,
                               mask4[64 * g:64 * g + 64, :], CB // 2)
                        piece += 1
                lo(c, 3)
                with dve.Fori(1, FULL) as f:
                    for g in range(2):
                        dve.wait_ge(hi_done[g], nth(c, 2) + f)
                        tt(wlo[:, g, 0:KB + 1, :], raw[:, g, 0:KB + 1, :], f32(whi[:, g, 0:KB + 1, :]),
                           ALU.subtract).then_inc(lo_done[g], 1)
                        if g == 0:
                            dve.wait_ge(unit_done[1], nth(c, 2) + f)
                            gate_up(c, f - 1, full, ps[:, UP, :])
                u = 2 + GU - 1
                lo(c, u)
                dve.wait_ge(unit_done[1], nth(c, u - 1) + 1)
                gate_up(c, FULL - 1, full, ps[:, UP, :])
                lo(c, u + 1)
                lo(c, u + 2)
                gate_up(c, FULL, slice(0, REST), ps[REST:P, GATE, :])
                lo(c, u + 3)
                lo(c, U_DOWN)
                dve.wait_ge(unit_done[1], nth(c, U_DOWN - 1) + 1)
                lora_t(c, 4, ps[:, TDB, :], full, slice(0, TOK), 0, mask8[:, :], CB)
                lo(c, U_DOWN + 1)
                with dve.Fori(0, KB // 2 - 1) as h:
                    for par in range(2):
                        lb = h * 2 + par
                        for i in range(2):
                            dve.wait_ge(hi_done[i], nth(c, U_DOWN) + lb + 1)
                            tt(wlo[:, i, 0:HALF + i, :], raw[:, i, 0:HALF + i, :],
                               f32(whi[:, i, 0:HALF + i, :]), ALU.subtract).then_inc(lo_done[i], 1)
                            if i == 0:
                                residual(c, lb, par, (c * (KB // 2) + h) * 16 + 16)
                for lb in (KB - 2, KB - 1):
                    if lb == KB - 2:
                        lo(c, U_DOWN + 2 * (KB - 1))
                    residual(c, lb, lb % 2, (c * (KB // 2) + lb // 2) * 16 + 16)
                    if lb == KB - 2:
                        lo(c, U_DOWN + 2 * (KB - 1) + 1)

            dve.wait_ge(mask_ready, 1)
            dve.wait_ge(w3_in, 2 * 16 * B)
            tt(w3bd[:, :, :], w3bd[:, :, :], ident[:, :].unsqueeze(1).to_broadcast([P, PAIRS, P]),
               ALU.add).then_inc(w3_ready, 1)
            tt(mask[:, :, :], mask[:, :, :], len_f[:, :].unsqueeze(1).to_broadcast([P, KB, B]),
               ALU.is_lt).then_inc(mask_ready, 1)
            dve.wait_ge(mask_ready, 2)
            x1h = x1s[:, :, :, :].rearrange("p c l (b h) -> p l c b h", h=C)
            with dve.Fori(0, C // 2) as g:
                for j in range(2):
                    h = g * 2 + j
                    dve.wait_ge(conv_done, h + (1 + CREDIT_CONV))
                    dve.wait_ge(x2_done, h + (1 + CREDIT_Y - 2))
                    tt(yv[:, j, :, :], ps[:, j, 0:KB * B].rearrange("p (l b) -> p l b", b=B), mask[:, :, :],
                       ALU.mult).then_inc(y_done, 1)
                    dve.wait_ge(y_done, h + (1 + CREDIT_Y))
                    xh = x1h[:, :, :, :, h]
                    tt(xh, xh, yv[:, j, :, :].rearrange("p l (c b) -> p l c b", c=NCH),
                       ALU.add).then_inc(x2_done, 1)
            for n in range(PAIRS):
                dve.wait_ge(l3_done, n + 1)
                if n >= 2:
                    dve.wait_ge(out_stored[n % 2], 16 * (n // 2))
                ts(ostage[:, n % 2, :], ps[:, 4 + 2 * (n % 2):6 + 2 * (n % 2), :].rearrange("p a t -> p (a t)"),
                   bcol[:, n:n + 1], None, ALU.add).then_inc(out_ready, 1)


def blocks(a, n):
    return a.reshape(n, P, -1).transpose(1, 0, 2)


def kernel(x, itok_B_0_15, itok_B_2_6, itok_B_78_3631, itok_B_0_31, L0_cond_weights, L1_cond_W_gate,
           L1_cond_W_up, L1_cond_W_down, L1_cond_A_gate, L1_cond_B_gate, L1_cond_A_up, L1_cond_B_up,
           L1_cond_A_down, L1_cond_B_down, L2_cond_log_dt, L2_cond_C, L2_cond_log_A_real, L2_cond_A_imag,
           L2_cond_D, L3_cond_weights, L3_cond_biases):
    import concourse.bacc as bacc
    from concourse.bass_utils import run_bass_kernel_spmd

    n = np.asarray
    cut = FULL * P

    def gate_up_blocks(gate, up, axis_rows):
        g, u = gate[:, :cut].reshape(-1, FULL, P), up[:, :cut].reshape(-1, FULL, P)
        return np.stack([g, u], 2).reshape(-1, 2 * FULL, P)

    wg, wu = n(L1_cond_W_gate).T, n(L1_cond_W_up).T
    w = np.concatenate([gate_up_blocks(wg, wu, T), np.concatenate([wg[:, cut:], wu[:, cut:]], 1)[:, None]], 1)
    wgu = w.reshape(KB, P, GU, P).transpose(2, 1, 0, 3)
    bg = n(L1_cond_B_gate)[0].transpose(0, 2, 1).reshape(NLORA * RANK, F)
    bu = n(L1_cond_B_up)[0].transpose(0, 2, 1).reshape(NLORA * RANK, F)
    zero = np.zeros((NLORA * RANK, REST), np.float32)
    bgu = np.concatenate([gate_up_blocks(bg, bu, 0).reshape(NLORA * RANK, -1), bg[:, cut:], zero, zero,
                          bu[:, cut:]], 1).reshape(NLORA, RANK, (GU + 1) * P)
    a = np.stack([n(L1_cond_A_gate)[0], n(L1_cond_A_up)[0]], 1)
    agu = a.reshape(NLORA, 2, RANK, KB, P).transpose(0, 4, 1, 3, 2).reshape(NLORA, P, -1)
    pad = FB * P - F
    ad = np.pad(n(L1_cond_A_down)[0], ((0, 0), (0, 0), (0, pad)))
    ad = ad.reshape(NLORA, RANK, FB, P).transpose(0, 3, 2, 1).reshape(NLORA, P, -1)
    wd = np.pad(n(L1_cond_W_down).T, ((0, pad), (0, 0)))
    wd = wd.reshape(2, HALF, P, KB, P).transpose(3, 0, 2, 1, 4)
    bd = n(L1_cond_B_down)[0].transpose(0, 2, 1)
    arrays = {
        "x": n(x).reshape(B * C, T), "cond": n(itok_B_0_15).reshape(1, B), "lora": n(itok_B_2_6).reshape(1, B),
        "length": n(itok_B_78_3631), "subj": n(itok_B_0_31).reshape(1, B),
        "w0": n(L0_cond_weights), "wgu": wgu, "wd": wd, "agu": agu, "ad": ad, "bgu": bgu, "bd": bd,
        "log_dt": n(L2_cond_log_dt), "c_ri": n(L2_cond_C).transpose(2, 1, 0), "log_ar": n(L2_cond_log_A_real).T,
        "a_im": n(L2_cond_A_imag).T, "d_skip": n(L2_cond_D).reshape(1, C),
        "w3": n(L3_cond_weights), "bias": n(L3_cond_biases).reshape(NSUBJ, C),
    }
    nc = bacc.Bacc("TRN2", target_bir_lowering=False, num_devices=1)
    arrays = {f"in_{k}": np.ascontiguousarray(v) for k, v in arrays.items()}
    aps = {k[3:]: nc.dram_tensor(k, v.shape, mybir.dt.from_np(v.dtype), kind="ExternalInput").ap()
           for k, v in arrays.items()}
    out = nc.dram_tensor("out", (B * C, T), F32, kind="ExternalOutput").ap()
    build(nc, out=out, **aps)
    r = run_bass_kernel_spmd(nc, [arrays], core_ids=[0])
    return r.results[0]["out"].reshape(B, C, T)
```

```python
from contextlib import ExitStack

import concourse.bass as bass
import numpy as np
from concourse import mybir

ALU = mybir.AluOpType
ACT = mybir.ActivationFunctionType
F32 = mybir.dt.float32
F32R = mybir.dt.float32r
I32 = mybir.dt.int32

P = 128
B, C, T = 32, 64, 1024
F, RANK = 2752, 16
NCOND, NLORA, NSUBJ = 16, 16, 32
NST = 64

NCH = 4
CB = B // NCH
TOK = CB * C
KB = T // P
PAIRS = B // 2
CP = CB // 2
FULL = F // P
REST = F - FULL * P
FB = FULL + 1
GU = 2 * FULL + 1
D0 = 12
HB = CB // 2
HT = TOK // 2
AD_UNITS = ((0, 8), (8, 15), (15, 22))
UNITS = 2 + GU + len(AD_UNITS) + 2 * KB
U_DOWN = 2 + GU + len(AD_UNITS)
US = UNITS // 2
assert REST * 2 == P and HB * RANK * 2 == P and UNITS % 2 == 0 and U_DOWN % 2 == 0 and TOK == 512

LS = 32
KROW = T + P
TRING, URING = 4, 4
ROUND = 1.5 * 2.0 ** 23
LN2_HI, LN2_LO = 0.693359375, -2.12194440e-4
CONSTS_KERNEL, CONSTS = 6, 16
KG_TH, KG_EXP, KG_SIN = 17, 24, 42
KG_UV = 83
TWO_PI = 6.283185


def build(nc, x, cond, lora, length, subj, w0, wgu, wd, agu, ad, bgu, bd, log_dt, c_ri, log_ar, a_im,
          d_skip, w3, bias, out):
    ctx = ExitStack()
    with ctx:
        def sem(name):
            return ctx.enter_context(nc.semaphore(name))

        def dram(name, shape):
            return nc.dram_tensor(name, shape, F32).ap()

        agu_of = dram("agu_of_batches", (NCH, P, CB * 2 * KB * RANK))
        ad_of = dram("ad_of_batches", (NCH, P, CB, FB * RANK))
        bgu_of = dram("bgu_of_batches", (NCH, P, GU + 1, 2, P))
        bd_of = dram("bd_of_batches", (NCH, P, KB, 2, P))
        x1_dram = dram("x1_dram", (NCH, P, KB, TOK))
        k_dram = dram("k_dram", (C, KROW))

        base = (nc.sbuf_base + 63) // 64 * 64

        def place(at, items):
            tiles = []
            for name, shape, dt in items:
                tiles.append(nc.alloc_sbuf_tensor_at(name, shape, dt, offset=at))
                at += (int(np.prod(shape[1:])) * 4 + 63) // 64 * 64
            assert at <= nc.sbuf_usable_end, (at, nc.sbuf_usable_end)
            return tiles, at

        (ids, ident, wbd, mask4, len_i, len_f, mask, bcol, ug), at = place(base, [
            ("ids", [1, 4, B], I32), ("ident", [P, P], F32), ("wbd", [P, PAIRS, P], F32),
            ("mask4", [P, HB], F32),
            ("len_i", [P, B], I32), ("len_f", [P, B], F32),
            ("mask", [P, KB, B], F32), ("bcol", [P, PAIRS], F32), ("ug", [P, URING, KB, B], F32)])
        stage_base = at
        (xn,), at = place(stage_base, [("xn", [P, CP, T], F32)])
        (t32, silu, act32, x1out, spare), at = place(at, [
            ("t32", [P, TOK], F32), ("silu", [P, TOK], F32), ("act32", [P, TOK], F32),
            ("x1out", [P, 2, TOK], F32), ("spare", [P, KB - 5, TOK], F32)])
        (xlo, xhi), raw_base = place(at, [("xlo", [P, KB, TOK], F32R), ("xhi", [P, KB, TOK], F32R)])
        (x1s,), end = place(stage_base, [("x1s", [P, NCH, KB, TOK], F32)])
        assert end == raw_base
        (raw, whi, wlo, t_hl), at = place(raw_base, [
            ("raw", [P, 2, 12, P], F32), ("whi", [P, 2, 12, P], F32R), ("wlo", [P, 2, 12, P], F32R),
            ("t_hl", [P, 2, 2, HT], F32R)])
        act_base = at
        (act_hi, act_lo), at = place(act_base, [
            ("act_hi", [P, FB, TOK], F32R), ("act_lo", [P, FULL, TOK], F32R)])
        small = "aim cre cim adt w1 w2 adt32 wc tmp th s1 c1 sh em er ei n2 qr qi cr ci al be".split()
        sm, at = place(act_base, [("s4_" + n, [P, C], F32) for n in small])
        s = dict(zip(small, sm))
        (ex_x, ex_k, ex_r, ex_p, ex_t, ex_i), at = place(at, [
            (n, [P, 2, C], I32 if n == "ex_i" else F32) for n in "ex_x ex_k ex_r ex_p ex_t ex_i".split()])
        s |= {"dt_": ex_x[:, 0, :], "ea": ex_x[:, 1, :]}
        (jj, ph, drow, last, dexp, vv, ve, uu, ue, ux, rr, ksb, kzero), _ = place(at, [
            ("jj", [P, LS], F32), ("ph", [P, 1], F32), ("drow", [1, C], F32),
            ("last", [1, LS], F32), ("dexp", [1, C, LS], F32),
            ("vv", [P, C, LS], F32), ("ve", [P, C, LS], F32), ("uu", [P, C, LS], F32),
            ("ue", [P, C, LS], F32), ("ux", [P, C, LS], F32), ("rr", [P, C, LS], F32),
            ("ksb", [LS, C, LS], F32), ("kzero", [C, P], F32)])
        (rtoep, toep, yv, x2n, ostage), _ = place(raw_base, [
            ("rtoep", [P, TRING, T], F32), ("toep", [P, TRING, T], F32), ("yv", [P, 2, KB, B], F32),
            ("x2n", [P, 2, T], F32), ("ostage", [P, 2, T], F32)])
        RAW_TILES = 2 * 12 * P // T

        ps = ctx.enter_context(nc.psum_tensor("ps", [P, 8, 512], F32))
        GATE, UP, DOWN, TDB, L0B = 0, 1, 2, 6, 4

        ids_in = sem("ids_in")
        par_in = sem("par_in")
        consts = sem("consts")
        w0_in = sem("w0_in")
        w0_ready = sem("w0_ready")
        gathered = sem("gathered")
        kg = sem("kernel_step")
        k_stored = sem("k_stored")
        silu_table = sem("silu_table")
        x_in = [sem(f"x_in{q}") for q in range(CP)]
        l0_done = sem("l0_done")
        l0_hi = sem("l0_hi")
        l0_lo = sem("l0_lo")
        raw_in = [sem(f"raw_in{i}") for i in range(2)]
        hi_done = [sem(f"hi_done{i}") for i in range(2)]
        lo_done = [sem(f"lo_done{i}") for i in range(2)]
        unit_done = [sem(f"unit_done{i}") for i in range(2)]
        t_step = sem("t_step")
        t_ready = sem("t_ready")
        silu_done = sem("silu_done")
        mul_done = sem("mul_done")
        act_hi_done = sem("act_hi_done")
        act_done = sem("act_done")
        res_step = sem("res_step")
        x1_ready = sem("x1_ready")
        x1_stored = [sem(f"x1_stored{i}") for i in range(2)]
        mask_ready = sem("mask_ready")
        w3_in = sem("w3_in")
        w3_ready = sem("w3_ready")
        x1_in = sem("x1_in")
        toep_in = [sem(f"toep_in{i}") for i in range(TRING)]
        ug_ready = sem("ug_ready")
        toep_ready = sem("toep_ready")
        conv_done = sem("conv_done")
        y_done = sem("y_done")
        x2_done = sem("x2_done")
        turned = sem("turned")
        x2n_ready = sem("x2n_ready")
        l3_done = sem("l3_done")
        out_ready = sem("out_ready")
        out_stored = [sem(f"out_stored{i}") for i in range(2)]
        CREDIT_CONV, CREDIT_Y, CREDIT_X1 = TRING, 2, 2

        block = ctx.enter_context(nc.Block())

        def nth(c, u):
            return c * US + (u // 2 + 1)

        xr = x.rearrange("(c q p) t -> c p q t", c=NCH, q=CP)
        outr = out.rearrange("(n p) t -> n p t", p=P)

        def split_views(u):
            i = u % 2
            if u < 2:
                r = raw[:, i, 0:KB, :].rearrange("p a b -> p (a b)").rearrange(
                    "p (b g k r) -> p g b k r", b=HB, g=2, r=RANK)
                v = [t[:, i, 0:KB, :].rearrange("p k (g b r) -> p g b k r", g=2, r=RANK) for t in (whi, wlo)]
                return [(r[:, g], v[0][:, g], v[1][:, g]) for g in range(2)]
            if U_DOWN > u >= 2 + GU:
                k0, k1 = AD_UNITS[u - 2 - GU]
                n = k1 - k0
                r = raw[:, i, 0:n, :].rearrange("p a b -> p (a b)").rearrange(
                    "p (f b k r) -> p f b k r", f=2, b=HB, r=RANK)
                v = [t[:, i, 0:n, :].rearrange("p k (s b r) -> p s b k r", s=2, r=RANK) for t in (whi, wlo)]
                return [(r[:, f], v[f][:, 0], v[f][:, 1]) for f in range(2)]
            n = KB + 4 if u == 1 + GU else KB + 2 if u < U_DOWN else D0
            return [(raw[:, i, 0:n, :], whi[:, i, 0:n, :], wlo[:, i, 0:n, :])]

        @block.sync
        def _(sp):
            def load_x(c):
                for q in range(CP):
                    if not (isinstance(c, int) and c == 0):
                        sp.wait_ge(l0_done, (c - 1) * CP + q + 1)
                    sp.dma_start(xn[:, q, :], xr[c, :, q, :]).then_inc(x_in[q], 16)

            def load_unit(c, u, parts):
                i = u % 2
                sp.wait_ge(lo_done[i], nth(c, u))
                for dst, src in parts:
                    sp.dma_start(dst, src).then_inc(raw_in[i], 16)

            def flat(i, a, b):
                return raw[:, i, :, :].rearrange("p a b -> p (a b)")[:, a:b]

            def chunk(c, last):
                sp.wait_ge(gathered, (c * CB + CB) * 16 * 6)
                n = CB // 2 * 2 * KB * RANK
                for u in range(2):
                    load_unit(c, u, [(flat(u, g * n // 2, (g + 1) * n // 2),
                                      agu_of[c, :, u * n + g * n // 2:u * n + (g + 1) * n // 2])
                                     for g in range(2)])

                with sp.Fori(0, FULL) as f:
                    for g in range(2):
                        sp.wait_ge(lo_done[g], nth(c, 2) + f)
                        sp.dma_start(raw[:, g, 0:KB, :], wgu[2 * f + g]).then_inc(raw_in[g], 16)
                        sp.dma_start(raw[:, g, KB:KB + 2, :], bgu_of[c, :, bass.ds(2 * f + g, 1)].rearrange(
                            "p o f m -> p (o f) m")).then_inc(raw_in[g], 16)
                u = 2 + GU - 1
                load_unit(c, u, [(raw[:, 0, 0:KB, :], wgu[GU - 1]),
                                 (raw[:, 0, KB:KB + 4, :],
                                  bgu_of[c, :, GU - 1:GU + 1].rearrange("p o f m -> p (o f) m"))])
                for n, (k0, k1) in enumerate(AD_UNITS):
                    u = 2 + GU + n
                    w = (k1 - k0) * RANK
                    dst = flat(u % 2, 0, CB * w).rearrange("p (b w) -> p b w", w=w)
                    load_unit(c, u, [(dst[:, b:b + CB // 2, :],
                                      ad_of[c, :, b:b + CB // 2, k0 * RANK:k1 * RANK])
                                     for b in (0, CB // 2)])
                if not last:
                    load_x(c + 1)
                else:
                    sp.wait_ge(l0_done, NCH * CP)
                    for i in range(2):
                        sp.wait_ge(x1_stored[i], 16 + 16 * (NCH - 1) * KB // 2)
                    sp.dma_start(x1s[:, 0, :, :], x1_dram[0]).then_inc(x1_in, 16)

                def load_down(lb):
                    for i in range(2):
                        sp.wait_ge(lo_done[i], nth(c, U_DOWN) + lb)
                        if i == 0:
                            for k in (0, D0 // 2):
                                sp.dma_start(raw[:, 0, k:k + D0 // 2, :],
                                             wd[lb, :, k:k + D0 // 2, :]).then_inc(raw_in[0], 16)
                        else:
                            sp.dma_start(raw[:, 1, 0:FB - D0, :], wd[lb, :, D0:FB, :]).then_inc(raw_in[1], 16)
                            sp.dma_start(raw[:, 1, FB - D0:D0, :], bd_of[c, :, bass.ds(lb, 1)].rearrange(
                                "p o f m -> p (o f) m")).then_inc(raw_in[1], 16)

                if not last:
                    with sp.Fori(0, KB) as lb:
                        load_down(lb)
                    return
                for lb in range(2):
                    load_down(lb)
                sp.wait_ge(t_ready, 1 + NCH * 5)
                sp.wait_ge(act_done, 1 + NCH * FB)
                sp.dma_start(x1s[:, 1, :, :], x1_dram[1]).then_inc(x1_in, 16)
                with sp.Fori(2, KB) as lb:
                    load_down(lb)

            load_x(0)
            with sp.Fori(0, NCH - 1) as c:
                chunk(c, False)
            chunk(NCH - 1, True)

            def load_x1(k0, k1):
                sp.wait_ge(x1_ready, CREDIT_X1 + (NCH - 1) * KB + k1)
                sp.dma_start(x1s[:, 2, k0:k1, :], x1_dram[2, :, k0:k1, :]).then_inc(x1_in, 16)

            kt = bass.AP(k_dram.tensor, 0, [[KROW, C], [1, P], [1, T]])

            def load_toep(h, j):
                sp.dma_start(rtoep[:, j, :], kt[h]).then_inc(toep_in[j], 16)

            load_x1(0, KB - 2)
            load_x1(KB - 2, KB - 1)
            sp.wait_ge(k_stored, 32)
            for i in range(2):
                sp.wait_ge(lo_done[i], 1 + NCH * US)
            for j in range(RAW_TILES):
                load_toep(j, j)
            load_x1(KB - 1, KB)
            sp.wait_ge(unit_done[1], 1 + NCH * US)
            for j in range(RAW_TILES, TRING):
                load_toep(j, j)
            with sp.Fori(1, C // TRING) as g:
                for j in range(TRING):
                    sp.wait_ge(toep_ready, g * TRING + (j + 1))
                    load_toep(g * TRING + j, j)
            for n in range(PAIRS):
                sp.wait_ge(out_ready, n + 1)
                sp.dma_start(outr[n], ostage[:, n % 2, :]).then_inc(out_stored[n % 2], 16)
            for i in range(2):
                sp.wait_ge(out_stored[i], 16 * PAIRS // 2)

        @block.gpsimd
        def _(pool):
            pool.dma_start(ids[0:1, 0, :], cond).then_inc(ids_in, 16)
            pool.dma_start(ids[0:1, 1, :], lora).then_inc(ids_in, 16)
            pool.dma_start(ids[0:1, 2, :], subj).then_inc(ids_in, 16)
            made = [0]

            def const(ins):
                ins.then_inc(consts, 1)
                made[0] += 1
                pool.wait_ge(consts, made[0])

            def select(tile, op, fill, base, pattern, m):
                const(pool.affine_select(out=tile, in_=tile, compare_op=op, fill=fill, base=base,
                                         pattern=pattern, channel_multiplier=m))
            const(pool.iota(jj[:, :], pattern=[[-1, LS]], base=LS - 1, channel_multiplier=0,
                            allow_small_or_imprecise_dtypes=True))
            const(pool.memset(ph[0:C, :], 0.25))
            const(pool.memset(ph[C:P, :], 0.0))
            const(pool.memset(last[:, :], 0.0))
            const(pool.memset(last[0:1, LS - 1:LS], 1.0))
            const(pool.memset(dexp[:, :, :], 0.0))
            assert made[0] == CONSTS_KERNEL
            const(pool.memset(ident[:, :], 0.0))
            select(ident[:, :], ALU.not_equal, 1.0, 0, [[-1, P]], 1)
            for m in (mask4[0:64, :], mask4[64:P, :]):
                const(pool.memset(m, 0.5))
                select(m, ALU.is_ge, 0.0, 0, [[-RANK, HB]], 1)
                select(m, ALU.is_ge, 0.0, RANK - 1, [[RANK, HB]], -1)
            const(pool.memset(kzero[:, :], 0.0))
            const(pool.memset(wbd[:, :, :], 0.0))
            assert made[0] == CONSTS
            pool.wait_ge(ids_in, 48)
            wv = wbd[:, :, :].rearrange("p n (g d) -> p n g d", g=2)
            with pool.Fori(0, PAIRS) as n:
                for g in range(2):
                    k = pool.value_load(ids[0:1, 0, bass.ds(2 * n + g, 1)], min_val=0, max_val=NCOND - 1)
                    pool.dma_start(wv[64 * g:64 * g + 64, bass.ds(n, 1), g, :],
                                   w0[bass.ds(k, 1)].rearrange("o c d -> c o d")).then_inc(w0_in, 16)
            with pool.Fori(0, NCH) as c:
                for half in range(2):
                    with pool.Fori(0, HB) as b:
                        k = pool.value_load(ids[0:1, 1, bass.ds(c * CB + b + half * HB, 1)], min_val=0,
                                            max_val=NLORA - 1)
                        wa = 2 * KB * RANK
                        pool.dma_start(agu_of[c, :, bass.ds((b + half * HB) * wa, wa)],
                                       agu[k]).then_inc(gathered, 16)
                        pool.dma_start(ad_of[c, :, b + half * HB, :], ad[k]).then_inc(gathered, 16)
                        for twice in range(2):
                            rows = bass.ds(b * RANK + twice * HB * RANK, RANK)
                            pool.dma_start(bgu_of[c, rows, :, half, :], bgu[k]).then_inc(gathered, 16)
                            pool.dma_start(bd_of[c, rows, :, half, :], bd[k]).then_inc(gathered, 16)
                pool.wait_ge(gathered, (c * CB + CB) * 16 * 6)
            pool.iota(mask[:, :, :], pattern=[[P, KB], [0, B]], base=0, channel_multiplier=1,
                      allow_small_or_imprecise_dtypes=True).then_inc(mask_ready, 1)
            pool.wait_ge(l0_done, NCH * CP)
            with pool.Fori(0, PAIRS) as n:
                for g in range(2):
                    k = pool.value_load(ids[0:1, 2, bass.ds(2 * n + g, 1)], min_val=0, max_val=NSUBJ - 1)
                    pool.dma_start(wv[64 * g:64 * g + 64, bass.ds(n, 1), g, :],
                                   w3[bass.ds(k, 1)].rearrange("o c d -> c o d")).then_inc(w3_in, 16)
                    pool.dma_start(bcol[64 * g:64 * g + 64, bass.ds(n, 1)],
                                   bias[bass.ds(k, 1), :].rearrange("o d -> d o")).then_inc(w3_in, 16)
            pool.wait_ge(w3_in, 2 * 16 * B)
            pool.tensor_tensor(wbd[:, :, :], wbd[:, :, :], ident[:, :].unsqueeze(1).to_broadcast([P, PAIRS, P]),
                               ALU.add).then_inc(w3_ready, 1)
            pool.wait_ge(x1_in, 16 * 5)
            pool.wait_ge(x1_ready, CREDIT_X1 + NCH * KB)
            x1h = x1s[:, :, :, :].rearrange("p c l (b h) -> p l c b h", h=C)
            with pool.Fori(0, C // URING) as g:
                for j in range(URING):
                    pool.wait_ge(conv_done, g * URING + (j + 1 - URING + CREDIT_CONV))
                    pool.tensor_copy(ug[:, j, :, :].rearrange("p l (c b) -> p l c b", c=NCH),
                                     x1h[:, :, :, :, g * URING + j]).then_inc(ug_ready, 1)

        @block.scalar
        def _(act):
            def load(dst, src):
                act.dma_start(dst, src).then_inc(par_in, 16)
            load(ex_x[:, 0, :], log_dt.partition_broadcast(P))
            load(drow[0:1, :], d_skip)
            load(len_i[:, :], length.partition_broadcast(P))
            for g in range(2):
                rows = slice(64 * g, 64 * g + 64)
                load(ex_x[rows, 1, :], log_ar)
                load(s["aim"][rows, :], a_im)
                load(s["cre"][rows, :], c_ri[0])
                load(s["cim"][rows, :], c_ri[1])
            act.wait_ge(par_in, 11 * 16)

            def fn(dst, src, f, scale=1.0):
                act.activation(dst, src, f, scale=scale).then_inc(kg, 1)
            act.wait_ge(kg, KG_TH)
            fn(s["th"][:, :], s["adt"][:, :], ACT.Tanh, 0.5)
            act.wait_ge(kg, KG_EXP)
            fn(ve[:, :, :], ve[:, :, :], ACT.Exp)
            fn(ue[:, :, :], ue[:, :, :], ACT.Exp)
            act.wait_ge(kg, KG_SIN)
            fn(s["s1"][:, :], s["w1"][:, :], ACT.Sin, TWO_PI)
            fn(s["c1"][:, :], s["wc"][:, :], ACT.Sin, TWO_PI)
            fn(s["sh"][:, :], s["w1"][:, :], ACT.Sin, TWO_PI / 2)
            fn(vv[:, :, :], vv[:, :, :], ACT.Sin, TWO_PI)
            fn(uu[:, :, :], uu[:, :, :], ACT.Sin, TWO_PI)
            fn(ux[:, :, :], ux[:, :, :], ACT.Sin, TWO_PI)

            act.wait_ge(kg, KG_UV + 2)
            act.dma_start(k_dram[:, T:KROW], kzero[:, :]).then_inc(k_stored, 16)
            act.dma_start(k_dram[:, 0:T].rearrange("h (a j) -> a h j", j=LS), ksb[:, :, :]).then_inc(k_stored, 16)

            def hi(c, u):
                i = u % 2
                n = nth(c, u)
                act.wait_ge(raw_in[i], n * 32)
                act.wait_ge(unit_done[i], n)
                for r, w_hi, _ in split_views(u):
                    ins = act.activation(w_hi, r, ACT.Copy)
                ins.then_inc(hi_done[i], 1)

            act.activation(silu[0:1, 0:1], drow[0:1, 0:1], ACT.Silu).then_inc(silu_table, 1)
            act.wait_ge(silu_table, 1)
            def chunk(c, last):
                hi(c, 0)
                hi(c, 1)
                act.wait_ge(x1_ready, c * KB + CREDIT_X1)
                for q in range(CP):
                    act.wait_ge(l0_done, c * CP + q + 1)
                    b = L0B + 2 * (q % 2)
                    act.activation(xhi[:, :, q * P:(q + 1) * P],
                                   ps[:, b:b + 2, :].rearrange("p b (k m) -> p (b k) m", m=P),
                                   ACT.Copy).then_inc(l0_hi, 1)
                with act.Fori(0, FULL) as f:
                    for g in range(2):
                        act.wait_ge(raw_in[g], (nth(c, 2) + f) * 32)
                        act.wait_ge(unit_done[g], nth(c, 2) + f)
                        act.activation(whi[:, g, 0:KB + 2, :], raw[:, g, 0:KB + 2, :],
                                       ACT.Copy).then_inc(hi_done[g], 1)
                    act.wait_ge(unit_done[0], nth(c, 2) + f + 1)
                    act.wait_ge(mul_done, c * FB + f + 1)
                    act.activation(silu[:, :], ps[:, GATE, :], ACT.Silu).then_inc(silu_done, 1)
                u = 2 + GU - 1
                hi(c, u)
                hi(c, u + 1)
                act.wait_ge(unit_done[0], nth(c, u) + 1)
                act.wait_ge(mul_done, c * FB + FULL + 1)
                act.activation(silu[0:REST, :], ps[0:REST, GATE, :], ACT.Silu).then_inc(silu_done, 1)
                hi(c, u + 2)
                hi(c, u + 3)

                def store(lb, par):
                    if last:
                        return
                    act.wait_ge(x1_ready, c * KB + lb + (1 + CREDIT_X1))
                    act.dma_start(x1_dram[c, :, lb, :], x1out[:, par, :]).then_inc(x1_stored[par], 16)

                hi(c, U_DOWN)
                hi(c, U_DOWN + 1)
                with act.Fori(0, KB // 2 - 1) as h:
                    for par in range(2):
                        for i in range(2):
                            n = nth(c, U_DOWN) + h * 2 + (par + 1)
                            act.wait_ge(raw_in[i], n * 32)
                            act.wait_ge(unit_done[i], n)
                            act.activation(whi[:, i, :, :], raw[:, i, :, :], ACT.Copy).then_inc(hi_done[i], 1)
                        store(h * 2 + par, par)
                hi(c, UNITS - 2)
                hi(c, UNITS - 1)
                store(KB - 2, 0)
                store(KB - 1, 1)

            with act.Fori(0, NCH - 1) as c:
                chunk(c, False)
            chunk(NCH - 1, True)

            act.wait_ge(unit_done[1], 1 + NCH * US)
            with act.Fori(0, C // TRING) as g:
                for j in range(TRING):
                    act.wait_ge(toep_in[j], g * 16 + 16)
                    act.wait_ge(conv_done, g * TRING + (j + 1))
                    act.activation(toep[:, j, :], rtoep[:, j, ::-1], ACT.Copy).then_inc(toep_ready, 1)

            for n in range(PAIRS):
                act.wait_ge(turned, n + 1)
                if n >= 2:
                    act.wait_ge(l3_done, n - 1)
                b = 2 * (n % 2)
                act.activation(x2n[:, n % 2, :], ps[:, b:b + 2, :].rearrange("p a t -> p (a t)"),
                               ACT.Copy).then_inc(x2n_ready, 1)

        @block.tensor
        def _(pe):
            def products(bank, w, nblk, r_hi, r_lo, start, stop, first=0):
                for k in range(first, first + nblk):
                    for n, (wt, r) in enumerate(((whi, r_hi), (whi, r_lo), (wlo, r_hi))):
                        ins = pe.matmul(bank, wt[:, w, k, :], r(k), start=start and k == first and n == 0,
                                        stop=stop and k == first + nblk - 1 and n == 2)
                return ins

            pe.wait_ge(kg, KG_UV)
            per_bank = 512 // LS
            for h in range(C):
                hb = h % per_bank
                if hb == 0:
                    pe.matmul(ps[0:LS, h // per_bank, :], last[:, :],
                              dexp[:, h:h + per_bank, :].rearrange("p h j -> p (h j)"), start=True, stop=False)
                ins = pe.matmul(ps[0:LS, h // per_bank, hb * LS:(hb + 1) * LS], uu[:, h, :], vv[:, h, :],
                                start=False, stop=hb == per_bank - 1)
            ins.then_inc(kg, 1)

            pe.wait_ge(w0_ready, 1)
            with pe.Fori(0, NCH) as c:
                pe.wait_ge(x1_ready, c * KB + CREDIT_X1)
                for q in range(CP):
                    pe.wait_ge(x_in[q], c * 16 + 16)
                    if q >= 2:
                        pe.wait_ge(l0_lo, c * CP + q - 1)
                    b = L0B + 2 * (q % 2)
                    for k in range(KB):
                        ins = pe.matmul(ps[:, b + k // 4, (k % 4) * P:(k % 4) * P + P],
                                        xn[:, q, k * P:(k + 1) * P],
                                        wbd[:, bass.ds(c * CP + q, 1), :].rearrange("p o d -> p (o d)"),
                                        start=True, stop=True)
                    ins.then_inc(l0_done, 1)
                for u in range(2):
                    pe.wait_ge(l0_lo, c * CP + 2 * u + 2)
                    pe.wait_ge(lo_done[u], nth(c, u) + 1)
                    t0 = u * TOK // 2
                    products(ps[:, DOWN + u, 0:TOK // 2], u, KB, lambda k: xhi[:, k, t0:t0 + TOK // 2],
                             lambda k: xlo[:, k, t0:t0 + TOK // 2], True, True).then_inc(unit_done[u], 1)

                def x_hi(k):
                    return xhi[:, k, :]

                def x_lo(k):
                    return xlo[:, k, :]

                def lora_b(bank, w, k, g, stop=True):
                    for half in range(2):
                        for n, wt in enumerate((whi, wlo)):
                            ins = pe.matmul(bank[:, half * HT:half * HT + HT], wt[:, w, k + half, :],
                                            t_hl[:, g, half, :], start=False, stop=stop and half == 1 and n == 1)
                    return ins

                with pe.Fori(0, FULL) as f:
                    pe.wait_ge(silu_done, c * FB + f + 1)
                    pe.wait_ge(lo_done[0], nth(c, 2) + f + 1)
                    products(ps[:, GATE, :], 0, KB, x_hi, x_lo, True, False)
                    pe.wait_ge(t_ready, c * 5 + 5)
                    lora_b(ps[:, GATE, :], 0, KB, 0).then_inc(unit_done[0], 1)
                    pe.wait_ge(mul_done, c * FB + f + 1)
                    pe.wait_ge(lo_done[1], nth(c, 2) + f + 1)
                    products(ps[:, UP, :], 1, KB, x_hi, x_lo, True, False)
                    lora_b(ps[:, UP, :], 1, KB, 1).then_inc(unit_done[1], 1)
                u = 2 + GU - 1
                pe.wait_ge(silu_done, c * FB + FULL + 1)
                pe.wait_ge(lo_done[0], nth(c, u) + 1)
                products(ps[:, GATE, :], 0, KB, x_hi, x_lo, True, False)
                lora_b(ps[:, GATE, :], 0, KB, 0, stop=False)
                lora_b(ps[:, GATE, :], 0, KB + 2, 1).then_inc(unit_done[0], 1)
                for n, (k0, k1) in enumerate(AD_UNITS):
                    u = 2 + GU + n
                    pe.wait_ge(act_done, c * FB + k1 + 1)
                    pe.wait_ge(lo_done[u % 2], nth(c, u) + 1)
                    for k in range(k0, k1):
                        for half in range(2):
                            w = (whi, wlo)[half][:, u % 2, k - k0, :]
                            cols = slice(half * HT, half * HT + HT)
                            ins = pe.matmul(ps[:, TDB + half, 0:HT], w, act_hi[:, k, cols], start=k == 0,
                                            stop=k == FULL)
                            if k < FULL:
                                ins = pe.matmul(ps[0:P // 2, TDB + half, 0:HT], w[:, 0:P // 2], act_lo[:, k, cols],
                                                start=False, stop=False)
                    ins.then_inc(unit_done[u % 2], 1)
                with pe.Fori(0, KB // 2) as h:
                    for par in range(2):
                        bank = ps[:, DOWN + par, :]
                        n = nth(c, U_DOWN) + h * 2 + par
                        pe.wait_ge(x1_ready, c * KB + h * 2 + (par + CREDIT_X1 - 1))
                        pe.wait_ge(lo_done[0], n + 1)
                        products(bank, 0, D0, lambda k: act_hi[:, k, :], lambda k: act_lo[:, k, :],
                                 True, False).then_inc(unit_done[0], 1)
                        pe.wait_ge(lo_done[1], n + 1)
                        products(bank, 1, FULL - D0, lambda k: act_hi[:, D0 + k, :],
                                 lambda k: act_lo[:, D0 + k, :], False, False)
                        for wt in (whi, wlo):
                            pe.matmul(bank, wt[:, 1, FULL - D0, :], act_hi[:, FULL, :], start=False, stop=False)
                        pe.wait_ge(t_ready, c * 5 + 6)
                        lora_b(bank, 1, FB - D0, 0).then_inc(unit_done[1], 1)

            with pe.Fori(0, C // TRING) as g:
                for j in range(TRING):
                    h = g * TRING + j
                    pe.wait_ge(toep_ready, h + (1 + TRING))
                    pe.wait_ge(ug_ready, h + 1)
                    pe.wait_ge(y_done, h + (1 + CREDIT_Y - 2))
                    y = ps[:, j % 2, 0:KB * B]
                    u = ug[:, j % URING, :, :].rearrange("p l b -> p (l b)")
                    for d in range(KB):
                        ins = pe.matmul(y[:, d * B:], toep[:, j, d * P:(d + 1) * P], u[:, 0:(KB - d) * B],
                                        start=d == 0, stop=d == KB - 1)
                    ins.then_inc(conv_done, 1)

            pe.wait_ge(x2_done, C + CREDIT_Y)
            pe.wait_ge(w3_ready, 1)

            def turn(n):
                if n >= 2:
                    pe.wait_ge(x2n_ready, n - 1)
                for k in range(KB):
                    ins = pe.transpose(ps[:, 2 * (n % 2) + k // 4, (k % 4) * P:(k % 4) * P + P],
                                       x1s[:, n // CP, k, (n % CP) * P:(n % CP) * P + P], ident[:, :])
                ins.then_inc(turned, 1)

            turn(0)
            for n in range(PAIRS):
                if n + 1 < PAIRS:
                    turn(n + 1)
                pe.wait_ge(x2n_ready, n + 1)
                if n >= 2:
                    pe.wait_ge(out_ready, n - 1)
                for k in range(2):
                    ins = pe.matmul(ps[:, 4 + 2 * (n % 2) + k, :], wbd[:, n, :],
                                    x2n[:, n % 2, k * 512:(k + 1) * 512], start=True, stop=True)
                ins.then_inc(l3_done, 1)

        @block.vector
        def _(dve):
            for i in range(2):
                dve.sem_inc(lo_done[i], 1)
                dve.sem_inc(unit_done[i], 1)
                dve.sem_inc(x1_stored[i], 16)
            dve.sem_inc(silu_done, 1)
            dve.sem_inc(mul_done, 1)
            dve.sem_inc(act_done, 1)
            dve.sem_inc(t_ready, 1)
            dve.sem_inc(x2_done, CREDIT_Y)
            dve.sem_inc(x1_ready, CREDIT_X1)
            dve.sem_inc(conv_done, CREDIT_CONV)
            dve.sem_inc(toep_ready, TRING)
            dve.sem_inc(y_done, CREDIT_Y)

            step = [0]

            def did(ins):
                ins.then_inc(kg, 1)
                step[0] += 1

            def after(n=None):
                dve.wait_ge(kg, step[0] if n is None else n)

            def per_h(t):
                return t[:, :].unsqueeze(2).to_broadcast([P, C, LS])

            powers = jj[:, :].unsqueeze(1).to_broadcast([P, C, LS])
            tt, ts, stt = dve.tensor_tensor, dve.tensor_scalar, dve.scalar_tensor_tensor

            def a(n):
                return s[n][:, :]

            dve.wait_ge(consts, CONSTS_KERNEL)
            dve.wait_ge(par_in, 11 * 16)
            dve.tensor_copy(len_f[:, :], len_i[:, :]).then_inc(t_step, 1)
            did(dve.tensor_copy(dexp[:, :, LS - 1], drow[:, :]))
            xe, ke, re_, pe_, te = (t[:, :, :] for t in (ex_x, ex_k, ex_r, ex_p, ex_t))
            did(ts(ke, xe, float(1 / np.log(2)), None, ALU.mult))
            after()
            did(ts(te, ke, ROUND, -ROUND, ALU.add, ALU.add))
            after()
            did(ts(ke, te, -126.0, 127.0, ALU.max, ALU.min))
            after()
            did(stt(re_, ke, -LN2_HI, xe, ALU.mult, ALU.add))
            after()
            did(stt(re_, ke, -LN2_LO, re_, ALU.mult, ALU.add))
            did(ts(te, ke, 127.0, 2.0 ** 23, ALU.add, ALU.mult))
            after()
            did(dve.tensor_copy(ex_i[:, :, :], te))
            did(ts(pe_, re_, 1 / 5040, None, ALU.mult))
            for k in (720, 120, 24, 6, 2, 1):
                after()
                did(stt(pe_, pe_, 1 / k, re_, ALU.add, ALU.mult))
            after()
            did(stt(ex_x[:, :, :], pe_, 1.0, ex_i[:, :, :].bitcast(F32), ALU.add, ALU.mult))
            after()
            did(stt(a("adt"), a("ea"), -1.0, a("dt_"), ALU.mult, ALU.mult))
            assert step[0] == KG_TH, step
            after()
            step[0] += 1
            did(ts(a("adt32"), a("adt"), float(LS), None, ALU.mult))
            did(tt(ve[:, :, :], per_h(s["adt"]), powers, ALU.mult))
            did(stt(a("w1"), a("aim"), 1 / (2 * np.pi), a("dt_"), ALU.mult, ALU.mult))
            after()
            did(tt(ue[:, :, :], per_h(s["adt32"]), powers, ALU.mult))
            did(ts(a("tmp"), a("w1"), ROUND, -ROUND, ALU.add, ALU.add))
            after()
            did(tt(a("w1"), a("w1"), a("tmp"), ALU.subtract))
            assert step[0] == KG_EXP, step
            after()
            step[0] += 2
            did(ts(a("w2"), a("w1"), float(LS), None, ALU.mult))
            did(ts(a("wc"), a("w1"), 0.25, None, ALU.add))
            did(tt(vv[:, :, :], per_h(s["w1"]), powers, ALU.mult))
            after()
            did(ts(a("tmp"), a("w2"), ROUND, -ROUND, ALU.add, ALU.add))
            did(ts(a("em"), a("wc"), ROUND, -ROUND, ALU.add, ALU.add))
            did(ts(vv[:, :, :], vv[:, :, :], ph[:, 0:1], None, ALU.add))
            after()
            did(tt(a("w2"), a("w2"), a("tmp"), ALU.subtract))
            did(tt(a("wc"), a("wc"), a("em"), ALU.subtract))
            did(ts(rr[:, :, :], vv[:, :, :], ROUND, -ROUND, ALU.add, ALU.add))
            after()
            did(tt(uu[:, :, :], per_h(s["w2"]), powers, ALU.mult))
            did(tt(vv[:, :, :], vv[:, :, :], rr[:, :, :], ALU.subtract))
            after()
            did(ts(ux[:, :, :], uu[:, :, :], 0.25, None, ALU.add))
            did(ts(rr[:, :, :], uu[:, :, :], ROUND, -ROUND, ALU.add, ALU.add))
            after()
            did(tt(uu[:, :, :], uu[:, :, :], rr[:, :, :], ALU.subtract))
            after()
            did(ts(rr[:, :, :], ux[:, :, :], ROUND, -ROUND, ALU.add, ALU.add))
            after()
            did(tt(ux[:, :, :], ux[:, :, :], rr[:, :, :], ALU.subtract))
            assert step[0] == KG_SIN, step
            step[0] += 6
            after()
            did(ts(a("tmp"), a("th"), -1.0, 1.0, ALU.mult, ALU.add))
            did(tt(a("sh"), a("sh"), a("sh"), ALU.mult))
            did(tt(a("n2"), a("ea"), a("ea"), ALU.mult))
            did(tt(a("cr"), a("aim"), a("aim"), ALU.mult))
            after()
            did(dve.reciprocal(a("tmp"), a("tmp")))
            did(tt(a("n2"), a("n2"), a("cr"), ALU.add))
            after()
            did(stt(a("em"), a("th"), 2.0, a("tmp"), ALU.mult, ALU.mult))
            did(dve.reciprocal(a("n2"), a("n2")))
            after()
            did(tt(a("er"), a("em"), a("c1"), ALU.mult))
            did(stt(a("ei"), a("em"), 1.0, a("s1"), ALU.add, ALU.mult))
            after()
            did(stt(a("er"), a("sh"), -2.0, a("er"), ALU.mult, ALU.add))
            after()
            did(tt(a("qr"), a("ei"), a("aim"), ALU.mult))
            did(tt(a("tmp"), a("er"), a("ea"), ALU.mult))
            did(tt(a("qi"), a("ei"), a("ea"), ALU.mult))
            did(tt(a("cr"), a("er"), a("aim"), ALU.mult))
            after()
            did(tt(a("qr"), a("qr"), a("tmp"), ALU.subtract))
            did(tt(a("qi"), a("qi"), a("cr"), ALU.add))
            after()
            did(tt(a("qr"), a("qr"), a("n2"), ALU.mult))
            did(stt(a("qi"), a("qi"), -1.0, a("n2"), ALU.mult, ALU.mult))
            after()
            did(tt(a("cr"), a("cre"), a("qr"), ALU.mult))
            did(tt(a("tmp"), a("cim"), a("qi"), ALU.mult))
            did(tt(a("ci"), a("cre"), a("qi"), ALU.mult))
            did(tt(a("er"), a("cim"), a("qr"), ALU.mult))
            after()
            did(tt(a("cr"), a("cr"), a("tmp"), ALU.subtract))
            did(tt(a("ci"), a("ci"), a("er"), ALU.add))
            after()
            did(ts(s["al"][0:C, :], s["cr"][0:C, :], 2.0, None, ALU.mult))
            did(ts(s["al"][C:P, :], s["ci"][C:P, :], -2.0, None, ALU.mult))
            did(ts(s["be"][0:C, :], s["ci"][0:C, :], -2.0, None, ALU.mult))
            did(ts(s["be"][C:P, :], s["cr"][C:P, :], -2.0, None, ALU.mult))
            did(tt(vv[:, :, :], vv[:, :, :], ve[:, :, :], ALU.mult))
            did(tt(uu[:, :, :], uu[:, :, :], ue[:, :, :], ALU.mult))
            did(tt(ux[:, :, :], ux[:, :, :], ue[:, :, :], ALU.mult))
            after()
            did(tt(uu[:, :, :], uu[:, :, :], per_h(s["be"]), ALU.mult))
            did(tt(ux[:, :, :], ux[:, :, :], per_h(s["al"]), ALU.mult))
            after()
            did(tt(uu[:, :, :], uu[:, :, :], ux[:, :, :], ALU.add))
            assert step[0] == KG_UV, step
            dve.wait_ge(consts, CONSTS)
            dve.wait_ge(w0_in, 16 * B)
            tt(wbd[:, :, :], wbd[:, :, :], ident[:, :].unsqueeze(1).to_broadcast([P, PAIRS, P]),
               ALU.add).then_inc(w0_ready, 1)
            step[0] += 1
            after()
            did(dve.tensor_copy(ksb[:, :, :].rearrange("p h j -> p (h j)"),
                                ps[0:LS, 0:4, :].rearrange("p a b -> p (a b)")))
            dve.wait_ge(k_stored, 32)

            def f32(t):
                return t.bitcast(F32)

            def lo(c, u):
                i = u % 2
                dve.wait_ge(hi_done[i], nth(c, u))
                for r, w_hi, w_lo in split_views(u):
                    ins = tt(w_lo, r, f32(w_hi), ALU.subtract)
                ins.then_inc(lo_done[i], 1)

            TS0 = 1
            TSC = 10

            def lora_t_gate_up(c, u):
                n = c * TSC + TS0 + 3 * u
                dve.wait_ge(t_ready, c * 5 + 1)
                cols = slice(u * HT, u * HT + HT)
                tt(t32[:, cols].rearrange("p (b n) -> p b n", n=C),
                   ps[:, DOWN + u, 0:HT].rearrange("p (b n) -> p b n", n=C),
                   mask4[:, :].unsqueeze(2).to_broadcast([P, HB, C]), ALU.mult).then_inc(t_step, 1)
                dve.wait_ge(t_step, n + 1)
                for g in range(2):
                    mine = slice(64 * g, 64 * g + 64)
                    dve.tensor_copy(t_hl[mine, g, u, :], t32[mine, cols]).then_inc(t_step, 1)
                for g in range(2):
                    mine, other = slice(64 * g, 64 * g + 64), slice(64 - 64 * g, P - 64 * g)
                    dve.wait_ge(t_step, n + 2 + g)
                    tt(t_hl[other, g, u, :], t32[mine, cols], f32(t_hl[mine, g, u, :]),
                       ALU.subtract).then_inc(t_ready, 1)

            def lora_t_down(c):
                n = c * TSC + TS0 + 6
                top = t32[0:64, :]
                halves = top.rearrange("p (f n) -> p f n", n=HT)
                dve.wait_ge(t_ready, c * 5 + 5)
                dve.tensor_copy(halves, ps[64:P, TDB:TDB + 2, 0:HT]).then_inc(t_step, 1)
                dve.wait_ge(t_step, n + 1)
                tt(halves, halves, ps[0:64, TDB:TDB + 2, 0:HT], ALU.add).then_inc(t_step, 1)
                dve.wait_ge(t_step, n + 2)
                by_batch = top.rearrange("p (f b n) -> p f b n", f=2, n=C)
                tt(by_batch, by_batch, mask4[0:64, :].unsqueeze(1).unsqueeze(3).to_broadcast([64, 2, HB, C]),
                   ALU.mult).then_inc(t_step, 1)
                dve.wait_ge(t_step, n + 3)
                dve.tensor_copy(t_hl[0:64, 0, :, :], halves).then_inc(t_step, 1)
                dve.wait_ge(t_step, n + 4)
                tt(t_hl[64:P, 0, :, :], halves, f32(t_hl[0:64, 0, :, :]), ALU.subtract).then_inc(t_ready, 1)

            full = slice(0, P)

            def gate_up(c, f, rows, up):
                n = c * FB + f
                dve.wait_ge(silu_done, n + 2)
                dve.wait_ge(act_done, n + 1)
                tt(act32[rows, :], silu[rows, :], up, ALU.mult).then_inc(mul_done, 1)
                dve.wait_ge(mul_done, n + 2)
                if rows == full:
                    a_hi, a_lo = (t[:, bass.ds(f, 1), :].rearrange("p o t -> p (o t)") for t in (act_hi, act_lo))
                else:
                    a_hi, a_lo = act_hi[rows, FULL, :], act_hi[REST:P, FULL, :]
                dve.tensor_copy(a_hi, act32[rows, :]).then_inc(act_hi_done, 1)
                dve.wait_ge(act_hi_done, n + 1)
                tt(a_lo, act32[rows, :], f32(a_hi), ALU.subtract).then_inc(act_done, 1)

            def residual(c, lb, par, last):
                dve.wait_ge(unit_done[1], nth(c, U_DOWN + 1) + lb + 1)
                if last:
                    o = x1s[:, NCH - 1, bass.ds(lb, 1), :].rearrange("p o t -> p (o t)")
                else:
                    dve.wait_ge(x1_stored[par], c * (KB // 2 * 16) + (lb - par) * 8 + 16)
                    o = x1out[:, par, :]
                tt(o, ps[:, DOWN + par, :], f32(xhi[:, bass.ds(lb, 1), :]).rearrange("p o t -> p (o t)"),
                   ALU.add).then_inc(res_step, 1)
                dve.wait_ge(res_step, c * KB + lb + 1)
                tt(o, o, f32(xlo[:, bass.ds(lb, 1), :]).rearrange("p o t -> p (o t)"),
                   ALU.add).then_inc(x1_ready, 1)

            def chunk(c, last):
                lo(c, 0)
                lo(c, 1)
                for q in range(CP):
                    dve.wait_ge(l0_hi, c * CP + q + 1)
                    b = L0B + 2 * (q % 2)
                    sl = slice(q * P, (q + 1) * P)
                    tt(xlo[:, :, sl], ps[:, b:b + 2, :].rearrange("p b (k m) -> p (b k) m", m=P),
                       f32(xhi[:, :, sl]), ALU.subtract).then_inc(l0_lo, 1)
                lo(c, 2)
                for u in range(2):
                    dve.wait_ge(unit_done[u], nth(c, u) + 1)
                    lora_t_gate_up(c, u)
                lo(c, 3)
                with dve.Fori(1, FULL) as f:
                    for g in range(2):
                        dve.wait_ge(hi_done[g], nth(c, 2) + f)
                        tt(wlo[:, g, 0:KB + 2, :], raw[:, g, 0:KB + 2, :], f32(whi[:, g, 0:KB + 2, :]),
                           ALU.subtract).then_inc(lo_done[g], 1)
                        if g == 0:
                            dve.wait_ge(unit_done[1], nth(c, 2) + f)
                            gate_up(c, f - 1, full, ps[:, UP, :])
                u = 2 + GU - 1
                lo(c, u)
                dve.wait_ge(unit_done[1], nth(c, u - 1) + 1)
                gate_up(c, FULL - 1, full, ps[:, UP, :])
                lo(c, u + 1)
                lo(c, u + 2)
                gate_up(c, FULL, slice(0, REST), ps[REST:P, GATE, :])
                lo(c, u + 3)
                lo(c, U_DOWN)
                dve.wait_ge(unit_done[1], nth(c, U_DOWN - 1) + 1)
                lora_t_down(c)
                lo(c, U_DOWN + 1)
                with dve.Fori(0, KB // 2 - 1) as h:
                    for par in range(2):
                        lb = h * 2 + par
                        for i in range(2):
                            dve.wait_ge(hi_done[i], nth(c, U_DOWN) + lb + 1)
                            tt(wlo[:, i, :, :], raw[:, i, :, :], f32(whi[:, i, :, :]), ALU.subtract).then_inc(lo_done[i], 1)
                            if i == 0:
                                residual(c, lb, par, last)
                for lb in (KB - 2, KB - 1):
                    if lb == KB - 2:
                        lo(c, U_DOWN + 2 * (KB - 1))
                    residual(c, lb, lb % 2, last)
                    if lb == KB - 2:
                        lo(c, U_DOWN + 2 * (KB - 1) + 1)

            with dve.Fori(0, NCH - 1) as c:
                chunk(c, False)
            dve.wait_ge(mask_ready, 1)
            tt(mask[:, :, :], mask[:, :, :], len_f[:, :].unsqueeze(1).to_broadcast([P, KB, B]),
               ALU.is_lt).then_inc(mask_ready, 1)
            chunk(NCH - 1, True)

            dve.wait_ge(mask_ready, 2)
            dve.wait_ge(x1_in, 16 * 5)
            x1h = x1s[:, :, :, :].rearrange("p c l (b h) -> p l c b h", h=C)
            with dve.Fori(0, C // 2) as g:
                for j in range(2):
                    h = g * 2 + j
                    dve.wait_ge(conv_done, h + (1 + CREDIT_CONV))
                    dve.wait_ge(x2_done, h + (1 + CREDIT_Y - 2))
                    tt(yv[:, j, :, :], ps[:, j, 0:KB * B].rearrange("p (l b) -> p l b", b=B), mask[:, :, :],
                       ALU.mult).then_inc(y_done, 1)
                    dve.wait_ge(y_done, h + (1 + CREDIT_Y))
                    xh = x1h[:, :, :, :, h]
                    tt(xh, xh, yv[:, j, :, :].rearrange("p l (c b) -> p l c b", c=NCH),
                       ALU.add).then_inc(x2_done, 1)
            for n in range(PAIRS):
                dve.wait_ge(l3_done, n + 1)
                if n >= 2:
                    dve.wait_ge(out_stored[n % 2], 16 * (n // 2))
                ts(ostage[:, n % 2, :], ps[:, 4 + 2 * (n % 2):6 + 2 * (n % 2), :].rearrange("p a t -> p (a t)"),
                   bcol[:, n:n + 1], None, ALU.add).then_inc(out_ready, 1)


def blocks(a, n):
    return a.reshape(n, P, -1).transpose(1, 0, 2)


def kernel(x, itok_B_0_15, itok_B_2_6, itok_B_78_3631, itok_B_0_31, L0_cond_weights, L1_cond_W_gate,
           L1_cond_W_up, L1_cond_W_down, L1_cond_A_gate, L1_cond_B_gate, L1_cond_A_up, L1_cond_B_up,
           L1_cond_A_down, L1_cond_B_down, L2_cond_log_dt, L2_cond_C, L2_cond_log_A_real, L2_cond_A_imag,
           L2_cond_D, L3_cond_weights, L3_cond_biases):
    import concourse.bacc as bacc
    from concourse.bass_utils import run_bass_kernel_spmd

    n = np.asarray
    cut = FULL * P

    def gate_up_blocks(gate, up, axis_rows):
        g, u = gate[:, :cut].reshape(-1, FULL, P), up[:, :cut].reshape(-1, FULL, P)
        return np.stack([g, u], 2).reshape(-1, 2 * FULL, P)

    wg, wu = n(L1_cond_W_gate).T, n(L1_cond_W_up).T
    w = np.concatenate([gate_up_blocks(wg, wu, T), np.concatenate([wg[:, cut:], wu[:, cut:]], 1)[:, None]], 1)
    wgu = w.reshape(KB, P, GU, P).transpose(2, 1, 0, 3)
    bg = n(L1_cond_B_gate)[0].transpose(0, 2, 1).reshape(NLORA * RANK, F)
    bu = n(L1_cond_B_up)[0].transpose(0, 2, 1).reshape(NLORA * RANK, F)
    zero = np.zeros((NLORA * RANK, REST), np.float32)
    bgu = np.concatenate([gate_up_blocks(bg, bu, 0).reshape(NLORA * RANK, -1), bg[:, cut:], zero, zero,
                          bu[:, cut:]], 1).reshape(NLORA, RANK, GU + 1, P)
    a = np.stack([n(L1_cond_A_gate)[0], n(L1_cond_A_up)[0]], 1)
    agu = a.reshape(NLORA, 2, RANK, KB, P).transpose(0, 4, 1, 3, 2).reshape(NLORA, P, -1)
    ad = n(L1_cond_A_down)[0]
    ad = np.concatenate([ad, ad[:, :, cut:]], 2)
    ad = ad.reshape(NLORA, RANK, FB, P).transpose(0, 3, 2, 1).reshape(NLORA, P, -1)
    wd = n(L1_cond_W_down).T
    wd = np.concatenate([wd, wd[cut:]], 0)
    wd = wd.reshape(FB, P, KB, P).transpose(2, 1, 0, 3)
    bd = n(L1_cond_B_down)[0].transpose(0, 2, 1).reshape(NLORA, RANK, KB, P)
    arrays = {
        "x": n(x).reshape(B * C, T), "cond": n(itok_B_0_15).reshape(1, B), "lora": n(itok_B_2_6).reshape(1, B),
        "length": n(itok_B_78_3631), "subj": n(itok_B_0_31).reshape(1, B),
        "w0": n(L0_cond_weights), "wgu": wgu, "wd": wd, "agu": agu, "ad": ad, "bgu": bgu, "bd": bd,
        "log_dt": n(L2_cond_log_dt), "c_ri": n(L2_cond_C).transpose(2, 1, 0), "log_ar": n(L2_cond_log_A_real).T,
        "a_im": n(L2_cond_A_imag).T, "d_skip": n(L2_cond_D).reshape(1, C),
        "w3": n(L3_cond_weights), "bias": n(L3_cond_biases).reshape(NSUBJ, C),
    }
    nc = bacc.Bacc("TRN2", target_bir_lowering=False, num_devices=1)
    arrays = {f"in_{k}": np.ascontiguousarray(v) for k, v in arrays.items()}
    aps = {k[3:]: nc.dram_tensor(k, v.shape, mybir.dt.from_np(v.dtype), kind="ExternalInput").ap()
           for k, v in arrays.items()}
    out = nc.dram_tensor("out", (B * C, T), F32, kind="ExternalOutput").ap()
    build(nc, out=out, **aps)
    r = run_bass_kernel_spmd(nc, [arrays], core_ids=[0])
    return r.results[0]["out"].reshape(B, C, T)
```

```python
from contextlib import ExitStack

import concourse.bass as bass
import numpy as np
from concourse import mybir

ALU = mybir.AluOpType
ACT = mybir.ActivationFunctionType
F32 = mybir.dt.float32
F32R = mybir.dt.float32r
I32 = mybir.dt.int32

P = 128
B, C, T = 32, 64, 1024
F, RANK = 2752, 16
NCOND, NLORA, NSUBJ = 16, 16, 32

NCH = 4
CB = B // NCH
TOK = CB * C
KB = T // P
PAIRS = B // 2
CP = CB // 2
FULL = F // P
REST = F - FULL * P
FB = FULL + 1
GU = 2 * FULL + 1
D0 = 12
HB = CB // 2
HT = TOK // 2
AD0_U, REST_U, AD1_U, DOWN0A_U, AD2_U, DOWN0B_U = range(2 + 2 * FULL, 8 + 2 * FULL)
AD_UNITS = {AD0_U: (0, 8), AD1_U: (8, 15), AD2_U: (15, FB)}
DOWN1_U = DOWN0B_U + 1
UNITS = DOWN1_U + 2 * (KB - 1)
PIECED = (0, 1, AD0_U, REST_U, AD1_U, DOWN0A_U, AD2_U, DOWN0B_U)
US = UNITS // 2
assert REST * 2 == P and HB * RANK * 2 == P and DOWN1_U % 2 == 0 and TOK == 512

LS = 32
KROW = T + P
TRING, URING = 4, 4
SPLIT = 2
TS = SPLIT * P
ROUND = 1.5 * 2.0 ** 23
LN2_HI, LN2_LO = 0.693359375, -2.12194440e-4
CONSTS_WBD, CONSTS = 3, 14
TAIL = FULL // 2 + 1
KG_TH, KG_U, KG_V, KG_UE, KG_VE = 23, 32, 36, 37, 38
KG_UV, KG_K = 73, 75
SP_BGU = 2
KA_ALL = 9
TWO_PI = 6.283185


def build(nc, x, cond, lora, length, subj, w0, wgu, wd, agu, ad, bgu, bd, log_dt, c_ri, log_ar, a_im,
          d_skip, w3, bias, out):
    ctx = ExitStack()
    with ctx:
        def sem(name):
            return ctx.enter_context(nc.semaphore(name))

        def dram(name, shape):
            return nc.dram_tensor(name, shape, F32).ap()

        agu_of = dram("agu_of_batches", (NCH, P, CB * 2 * KB * RANK))
        ad_of = dram("ad_of_batches", (NCH, P, CB, FB * RANK))
        bgu_of = dram("bgu_of_batches", (NCH, HB * RANK, GU + 1, 2, P))
        bd_of = dram("bd_of_batches", (NCH, HB * RANK, KB, 2, P))
        x1_dram = dram("x1_dram", (NCH, P, KB, TOK))
        k_dram = dram("k_dram", (C, KROW))

        base = (nc.sbuf_base + 63) // 64 * 64

        def place(at, items):
            tiles = []
            for name, shape, dt in items:
                tiles.append(nc.alloc_sbuf_tensor_at(name, shape, dt, offset=at))
                at += (int(np.prod(shape[1:])) * 4 + 63) // 64 * 64
            assert at <= nc.sbuf_usable_end, (at, nc.sbuf_usable_end)
            return tiles, at

        (ids, ident, wbd, mask4, len_i, len_f, mask, bcol, ug), at = place(base, [
            ("ids", [1, 4, B], I32), ("ident", [P, P], F32), ("wbd", [P, PAIRS, P], F32),
            ("mask4", [P, HB], F32),
            ("len_i", [P, B], I32), ("len_f", [P, B], F32),
            ("mask", [P, KB, B], F32), ("bcol", [P, PAIRS], F32), ("ug", [P, URING, KB, B], F32)])
        (jj, ph, e_last, dd, kzero), at = place(at, [
            ("jj", [P, LS], F32), ("ph", [P, 1], F32), ("e_last", [LS, 1], F32), ("dd", [LS, C], F32),
            ("kzero", [C, P], F32)])
        stage_base = at
        (xn,), at = place(stage_base, [("xn", [P, CP, T], F32)])
        (t32, silu, act32), x1out_base = place(at, [
            ("t32", [P, TOK], F32), ("silu", [P, TOK], F32), ("act32", [P, TOK], F32)])
        (x1out, spare), at = place(x1out_base, [
            ("x1out", [P, 2, TOK], F32), ("spare", [P, KB - 5, TOK], F32)])
        (xlo, xhi), raw_base = place(at, [("xlo", [P, KB, TOK], F32R), ("xhi", [P, KB, TOK], F32R)])
        (x1s,), end = place(stage_base, [("x1s", [P, NCH, KB, TOK], F32)])
        assert end == raw_base
        (raw, whi, wlo, t_hl), at = place(raw_base, [
            ("raw", [P, 2, 12, P], F32), ("whi", [P, 2, 12, P], F32R), ("wlo", [P, 2, 12, P], F32R),
            ("t_hl", [P, 2, 2, HT], F32R)])
        act_base = at
        (act_hi, act_lo), at = place(act_base, [
            ("act_hi", [P, FB, TOK], F32R), ("act_lo", [P, FULL, TOK], F32R)])
        small = "aim cre cim adt w1 w2 adt32 wc tmp th s1 c1 sh em er ei n2 qr qi cr ci al be".split()
        (uu, ux, *sm), at = place(act_base + TAIL * TOK * 4, [
            ("uu", [P, C, LS], F32), ("ux", [P, C, LS], F32)] + [("s4_" + n, [P, C], F32) for n in small])
        assert at <= act_base + FB * TOK * 4
        s = dict(zip(small, sm))
        (vv, ue, ex_x, ex_k, ex_r, ex_p, ex_t, ex_i), at = place(act_base + (FB + TAIL) * TOK * 4, [
            ("vv", [P, C, LS], F32), ("ue", [P, C, LS], F32)] + [
            (n, [P, 2, C], I32 if n == "ex_i" else F32) for n in "ex_x ex_k ex_r ex_p ex_t ex_i".split()])
        assert at <= act_base + (FB + FULL) * TOK * 4
        s |= {"dt_": ex_x[:, 0, :], "ea": ex_x[:, 1, :]}
        (ve,), _ = place(x1out_base, [("ve", [P, C, LS], F32)])
        (ksb,), _ = place(x1out_base, [("ksb", [LS, C, LS], F32)])

        (rtoep, toep, toep_h, toep_l, u_hl, yv, x2hi, x2lo, ostage, w3hi, w3lo), _ = place(raw_base, [
            ("rtoep", [P, TRING, T], F32), ("toep", [P, TRING, T], F32), ("toep_h", [P, TRING, TS], F32R),
            ("toep_l", [P, TRING, TS], F32R), ("u_hl", [P, URING, 2, KB * B], F32R), ("yv", [P, 2, KB, B], F32),
            ("x2hi", [P, 2, T], F32R), ("x2lo", [P, 2, T], F32R), ("ostage", [P, 2, T], F32),
            ("w3hi", [P, PAIRS, P], F32R), ("w3lo", [P, PAIRS, P], F32R)])
        RAW_TILES = 2 * 12 * P // T

        ps = ctx.enter_context(nc.psum_tensor("ps", [P, 8, 512], F32))
        GATE, UP, DOWN, TDB = 0, 1, 2, 6
        L0_BANKS = (4, 6, 0, 4)

        ids_in = sem("ids_in")
        par_in = sem("par_in")
        consts = sem("consts")
        w0_first_in = [sem(f"w0_first_in{g}") for g in range(2)]
        w0_in = sem("w0_in")
        w0_ready = [sem(f"w0_ready{i}") for i in range(2)]
        agu_in = [sem(f"agu_in{i}") for i in range(2)]
        bgu_in = [sem(f"bgu_in{i}") for i in range(2)]
        gathered = sem("gathered")
        kg = sem("kernel_step")
        ka = sem("kernel_step_act")
        kp = sem("kernel_step_pe")
        kzero_ready = sem("kzero_ready")
        k_stored = sem("k_stored")
        silu_table = sem("silu_table")
        x_in = [sem(f"x_in{q}") for q in range(CP)]
        l0_done = sem("l0_done")
        l0_hi = sem("l0_hi")
        l0_lo = sem("l0_lo")
        raw_in = [sem(f"raw_in{i}") for i in range(2)]
        hi_done = [sem(f"hi_done{i}") for i in range(2)]
        hi_first = sem("hi_first_piece")
        lo_done = [sem(f"lo_done{i}") for i in range(2)]
        unit_done = [sem(f"unit_done{i}") for i in range(2)]
        t_step = sem("t_step")
        t_ready = sem("t_ready")
        silu_done = sem("silu_done")
        mul_done = sem("mul_done")
        act_hi_done = sem("act_hi_done")
        act_done = sem("act_done")
        res_step = sem("res_step")
        x1_ready = sem("x1_ready")
        x1_stored = [sem(f"x1_stored{i}") for i in range(2)]
        mask_ready = sem("mask_ready")
        w3_in = sem("w3_in")
        w3_ready = sem("w3_ready")
        x1_in = sem("x1_in")
        toep_in = [sem(f"toep_in{i}") for i in range(TRING)]
        ug_ready = sem("ug_ready")
        toep_ready = sem("toep_ready")
        toep_hi = sem("toep_hi")
        toep_lo = sem("toep_lo")
        u_hi = sem("u_hi")
        u_lo = sem("u_lo")
        conv_done = sem("conv_done")
        y_done = sem("y_done")
        x2_done = sem("x2_done")
        turned = sem("turned")
        w3_hi = sem("w3_hi")
        w3_lo = sem("w3_lo")
        x2_hi = sem("x2_hi")
        x2_lo = sem("x2_lo")
        l3_done = sem("l3_done")
        out_ready = [sem(f"out_ready{i}") for i in range(2)]
        out_stored = [sem(f"out_stored{i}") for i in range(2)]
        CREDIT_CONV, CREDIT_Y, CREDIT_X1 = TRING, 2, 2

        block = ctx.enter_context(nc.Block())

        def nth(c, u):
            return c * US + (u // 2 + 1)

        xr = x.rearrange("(c q p) t -> c p q t", c=NCH, q=CP)
        outr = out.rearrange("(n p) t -> n p t", p=P)

        def split_views(u):
            i = u % 2
            if u < 2:
                r = raw[:, i, 0:KB, :].rearrange("p a b -> p (a b)").rearrange(
                    "p (b g k r) -> p g b k r", b=HB, g=2, r=RANK)
                v = [t[:, i, 0:KB, :].rearrange("p k (g b r) -> p g b k r", g=2, r=RANK) for t in (whi, wlo)]
                return [(r[:, g], v[0][:, g], v[1][:, g]) for g in range(2)]
            if u in AD_UNITS:
                k0, k1 = AD_UNITS[u]
                n = k1 - k0
                r = raw[:, i, 0:n, :].rearrange("p a b -> p (a b)").rearrange(
                    "p (f b k r) -> p f b k r", f=2, b=HB, r=RANK)
                v = [t[:, i, 0:n, :].rearrange("p k (s b r) -> p s b k r", s=2, r=RANK) for t in (whi, wlo)]
                return [(r[:, f], v[f][:, 0], v[f][:, 1]) for f in range(2)]
            n = KB + 2 if u < REST_U else D0
            pieces = (slice(0, n // 2), slice(n // 2, n)) if u in PIECED else (slice(0, n),)
            return [(raw[:, i, k, :], whi[:, i, k, :], wlo[:, i, k, :]) for k in pieces]

        def first_pieces(c, u):
            return c * len(PIECED) + PIECED.index(u) + 1

        @block.sync
        def _(sp):
            def load_x(c):
                for q in range(CP):
                    if not (isinstance(c, int) and c == 0):
                        sp.wait_ge(l0_done, (c - 1) * CP + q + 1)
                    sp.dma_start(xn[:, q, :], xr[c, :, q, :]).then_inc(x_in[q], 16)

            def load_unit(c, u, parts):
                i = u % 2
                sp.wait_ge(lo_done[i], nth(c, u))
                for dst, src in parts:
                    sp.dma_start(dst, src).then_inc(raw_in[i], 16)

            def flat(i, a, b):
                return raw[:, i, :, :].rearrange("p a b -> p (a b)")[:, a:b]

            def load_b(i, k, of, block):
                n = of.shape[1] if block is None else 2
                src = of if block is None else of[:, bass.ds(block, 1), :, :].rearrange("p o f m -> p (o f) m")
                for rows in (slice(0, 64), slice(64, P)):
                    sp.dma_start(raw[rows, i, k:k + n, :], src).then_inc(raw_in[i], 16)

            def gather_a_0():
                sp.wait_ge(ids_in, 48)
                wa = 2 * KB * RANK
                for b in range(HB):
                    k = sp.value_load(ids[0:1, 1, b:b + 1], min_val=0, max_val=NLORA - 1)
                    sp.dma_start(agu_of[0, :, b * wa:(b + 1) * wa], agu[k]).then_inc(agu_in[0], 16)

            def gather_b_0():
                for b in range(CB - SP_BGU, CB):
                    k = sp.value_load(ids[0:1, 1, b:b + 1], min_val=0, max_val=NLORA - 1)
                    rows = slice(b % HB * RANK, b % HB * RANK + RANK)
                    sp.dma_start(bgu_of[0, rows, :, b // HB, :], bgu[k]).then_inc(bgu_in[1], 16)

            def chunk(c, first, last):
                if not first:
                    sp.wait_ge(gathered, (c * CB * 4 + CB * 2) * 16)
                n = HB * 2 * KB * RANK
                for u in range(2):
                    if first and u == 1:
                        gather_b_0()
                    if first:
                        sp.wait_ge(agu_in[u], HB * 16)
                    load_unit(c, u, [(flat(u, a, b), agu_of[c, :, u * n + a:u * n + b])
                                     for a, b in ((0, n // 2), (n // 2, 3 * n // 4), (3 * n // 4, n))])
                if first:
                    sp.wait_ge(bgu_in[0], (CB - SP_BGU) * 16)
                    sp.wait_ge(bgu_in[1], SP_BGU * 16)
                with sp.Fori(0, FULL) as f:
                    for g in range(2):
                        sp.wait_ge(lo_done[g], nth(c, 2) + f)
                        sp.dma_start(raw[:, g, 0:KB, :], wgu[2 * f + g]).then_inc(raw_in[g], 16)
                        load_b(g, KB, bgu_of[c], 2 * f + g)

                def load_a_down(u):
                    k0, k1 = AD_UNITS[u]
                    w = (k1 - k0) * RANK
                    dst = flat(u % 2, 0, CB * w).rearrange("p (b w) -> p b w", w=w)
                    load_unit(c, u, [(dst[:, a:b, :], ad_of[c, :, a:b, k0 * RANK:k1 * RANK])
                                     for a, b in ((0, 3), (3, 6), (6, CB))])

                def load_down_a(i, lb):
                    for k in range(0, D0, D0 // 3):
                        sp.dma_start(raw[:, i, k:k + D0 // 3, :],
                                     wd[lb, :, k:k + D0 // 3, :]).then_inc(raw_in[i], 16)

                def load_down_b(i, lb):
                    sp.dma_start(raw[:, i, 0:FB - D0, :], wd[lb, :, D0:FB, :]).then_inc(raw_in[i], 16)
                    load_b(i, FB - D0, bd_of[c], lb)

                if first:
                    sp.wait_ge(gathered, CB * 2 * 16)
                load_a_down(AD0_U)
                i = REST_U % 2
                load_unit(c, REST_U, [(raw[:, i, 0:KB, :], wgu[GU - 1])])
                load_b(i, KB, bgu_of[c, :, GU - 1:GU + 1].rearrange("p o f m -> p (o f) m"), None)
                load_a_down(AD1_U)
                load_unit(c, DOWN0A_U, [])
                load_down_a(DOWN0A_U % 2, 0)
                load_a_down(AD2_U)
                load_unit(c, DOWN0B_U, [])
                load_down_b(DOWN0B_U % 2, 0)
                if not last:
                    load_x(c + 1)
                else:
                    sp.wait_ge(l0_done, NCH * CP)
                    for i in range(2):
                        sp.wait_ge(x1_stored[i], 16 + 16 * (NCH - 1) * KB // 2)
                    sp.dma_start(x1s[:, 0, :, :], x1_dram[0]).then_inc(x1_in, 16)

                def load_down(lb):
                    for i, load in enumerate((load_down_a, load_down_b)):
                        sp.wait_ge(lo_done[i], nth(c, DOWN1_U) + lb - 1)
                        load(i, lb)

                if not last:
                    with sp.Fori(1, KB) as lb:
                        load_down(lb)
                    return
                for lb in (1, 2):
                    load_down(lb)
                sp.wait_ge(t_ready, 1 + NCH * 5)
                sp.wait_ge(act_done, 1 + NCH * FB)
                sp.dma_start(x1s[:, 1, :, :], x1_dram[1]).then_inc(x1_in, 16)
                with sp.Fori(3, KB) as lb:
                    load_down(lb)

            for row, src in enumerate((cond, lora, subj)):
                sp.dma_start(ids[0:1, row, :], src).then_inc(ids_in, 16)
            load_x(0)
            gather_a_0()
            chunk(0, True, False)
            with sp.Fori(1, NCH - 1) as c:
                chunk(c, False, False)
            chunk(NCH - 1, False, True)

            def load_x1(k0, k1):
                sp.wait_ge(res_step, (NCH - 1) * KB + k1)
                sp.dma_start(x1s[:, 2, k0:k1, :], x1_dram[2, :, k0:k1, :]).then_inc(x1_in, 16)

            kt = bass.AP(k_dram.tensor, 0, [[KROW, C], [1, P], [1, T]])

            def load_toep(h, j):
                sp.dma_start(rtoep[:, j, :], kt[h]).then_inc(toep_in[j], 16)

            load_x1(0, KB - 2)
            load_x1(KB - 2, KB - 1)
            sp.wait_ge(k_stored, 32)
            for i in range(2):
                sp.wait_ge(lo_done[i], 1 + NCH * US)
            for j in range(RAW_TILES):
                load_toep(j, j)
            load_x1(KB - 1, KB)
            sp.wait_ge(unit_done[1], 1 + NCH * US)
            for j in range(RAW_TILES, TRING):
                load_toep(j, j)
            with sp.Fori(1, C // TRING) as g:
                for j in range(TRING):
                    sp.wait_ge(toep_ready, g * TRING + (j + 1))
                    sp.wait_ge(toep_lo, g * TRING + (j + 1))
                    load_toep(g * TRING + j, j)
            for n in range(PAIRS):
                for i in range(2):
                    sp.wait_ge(out_ready[i], n + 1)
                sp.dma_start(outr[n], ostage[:, n % 2, :]).then_inc(out_stored[n % 2], 16)
            for i in range(2):
                sp.wait_ge(out_stored[i], 16 * PAIRS // 2)

        @block.gpsimd
        def _(pool):
            made = [0]

            def const(ins):
                ins.then_inc(consts, 1)
                made[0] += 1
                pool.wait_ge(consts, made[0])

            def select(tile, op, fill, base, pattern, m):
                const(pool.affine_select(out=tile, in_=tile, compare_op=op, fill=fill, base=base,
                                         pattern=pattern, channel_multiplier=m))
            const(pool.memset(wbd[:, :, :], 0.0))
            const(pool.memset(ident[:, :], 0.0))
            select(ident[:, :], ALU.not_equal, 1.0, 0, [[-1, P]], 1)
            assert made[0] == CONSTS_WBD

            wv = wbd[:, :, :].rearrange("p n (g d) -> p n g d", g=2)

            def gather_w(n, g, key_row, table, landed):
                k = pool.value_load(ids[0:1, key_row, bass.ds(2 * n + g, 1)], min_val=0,
                                    max_val=table.shape[0] - 1)
                pool.dma_start(wv[64 * g:64 * g + 64, bass.ds(n, 1), g, :],
                               table[bass.ds(k, 1)].rearrange("o c d -> c o d")).then_inc(landed, 16)
                return k

            def add_identity(n0, n1):
                w = wbd[:, n0:n1, :]
                return pool.tensor_tensor(w, w, ident[:, :].unsqueeze(1).to_broadcast([P, n1 - n0, P]), ALU.add)

            def gather_b_gate_up(c, half, b, k, landed):
                pool.dma_start(bgu_of[c, bass.ds(b * RANK, RANK), :, half, :], bgu[k]).then_inc(landed, 16)

            def lora_key(c, half, b):
                return pool.value_load(ids[0:1, 1, bass.ds(c * CB + b + half * HB, 1)], min_val=0,
                                       max_val=NLORA - 1)

            def gather_lora(c, half, b, gate_up, down):
                k = lora_key(c, half, b)
                wa = 2 * KB * RANK
                rows = bass.ds(b * RANK, RANK)
                if gate_up:
                    pool.dma_start(agu_of[c, :, bass.ds((b + half * HB) * wa, wa)],
                                   agu[k]).then_inc(gathered, 16)
                    gather_b_gate_up(c, half, b, k, gathered)
                if down:
                    pool.dma_start(ad_of[c, :, b + half * HB, :], ad[k]).then_inc(gathered, 16)
                    pool.dma_start(bd_of[c, rows, :, half, :], bd[k]).then_inc(gathered, 16)

            pool.wait_ge(ids_in, 48)
            with pool.Fori(0, CP) as n:
                gather_w(n, 0, 0, w0, w0_first_in[0])
            for m in (mask4[0:64, :], mask4[64:P, :]):
                const(pool.memset(m, 0.5))
                select(m, ALU.is_ge, 0.0, 0, [[-RANK, HB]], 1)
                select(m, ALU.is_ge, 0.0, RANK - 1, [[RANK, HB]], -1)
            for half in range(2):
                with pool.Fori(0, HB - half * SP_BGU) as b:
                    gather_b_gate_up(0, half, b, lora_key(0, half, b), bgu_in[0])
            def load(dst, src):
                pool.dma_start(dst, src).then_inc(par_in, 16)

            load(ex_x[:, 0, :], log_dt.partition_broadcast(P))
            for g in range(2):
                rows = slice(64 * g, 64 * g + 64)
                load(ex_x[rows, 1, :], log_ar)
                load(s["aim"][rows, :], a_im)
                load(s["cre"][rows, :], c_ri[0])
                load(s["cim"][rows, :], c_ri[1])
            load(dd[:, :], d_skip.partition_broadcast(LS))
            load(len_i[:, :], length.partition_broadcast(P))
            const(pool.iota(jj[:, :], pattern=[[-1, LS]], base=LS - 1, channel_multiplier=0,
                            allow_small_or_imprecise_dtypes=True))
            const(pool.memset(ph[0:C, :], 0.25))
            const(pool.memset(ph[C:P, :], 0.0))
            const(pool.memset(e_last[:, :], 0.0))
            select(e_last[:, :], ALU.not_equal, 1.0, 1 - LS, [[0, 1]], 1)
            assert made[0] == CONSTS
            pool.memset(kzero[:, :], 0.0).then_inc(kzero_ready, 1)
            with pool.Fori(CP, PAIRS) as n:
                for g in range(2):
                    gather_w(n, g, 0, w0, w0_in)
            pool.wait_ge(w0_in, 16 * (B - CB))
            add_identity(CP, PAIRS).then_inc(w0_ready[1], 1)
            for half in range(2):
                with pool.Fori(0, HB) as b:
                    gather_lora(0, half, b, False, True)
            pool.wait_ge(gathered, CB * 2 * 16)
            pool.wait_ge(kzero_ready, 1)
            pool.dma_start(k_dram[:, T:KROW], kzero[:, :]).then_inc(k_stored, 16)
            pool.wait_ge(kg, KG_K)
            pool.dma_start(k_dram[:, 0:T].rearrange("h (a j) -> a h j", j=LS),
                           ksb[:, :, :]).then_inc(k_stored, 16)
            with pool.Fori(1, NCH) as c:
                for half in range(2):
                    with pool.Fori(0, HB) as b:
                        gather_lora(c, half, b, True, True)
                pool.wait_ge(gathered, (c * CB * 4 + CB * 2) * 16)
            pool.iota(mask[:, :, :], pattern=[[P, KB], [0, B]], base=0, channel_multiplier=1,
                      allow_small_or_imprecise_dtypes=True).then_inc(mask_ready, 1)
            pool.wait_ge(l0_done, NCH * CP)
            with pool.Fori(0, PAIRS) as n:
                for g in range(2):
                    k = gather_w(n, g, 2, w3, w3_in)
                    pool.dma_start(bcol[64 * g:64 * g + 64, bass.ds(n, 1)],
                                   bias[bass.ds(k, 1), :].rearrange("o d -> d o")).then_inc(w3_in, 16)
            pool.wait_ge(w3_in, 2 * 16 * B)
            add_identity(0, PAIRS).then_inc(w3_ready, 1)
            pool.wait_ge(x1_in, 16 * 5)
            pool.wait_ge(x1_ready, CREDIT_X1 + NCH * KB)
            x1h = x1s[:, :, :, :].rearrange("p c l (b h) -> p l c b h", h=C)
            with pool.Fori(0, C // URING) as g:
                for j in range(URING):
                    pool.wait_ge(conv_done, g * URING + (j + 1 - URING + CREDIT_CONV))
                    pool.tensor_copy(ug[:, j, :, :].rearrange("p l (c b) -> p l c b", c=NCH),
                                     x1h[:, :, :, :, g * URING + j]).then_inc(ug_ready, 1)
            pool.wait_ge(w3_hi, 1)
            pool.tensor_tensor(w3lo[:, :, :], wbd[:, :, :], w3hi[:, :, :].bitcast(F32),
                               ALU.subtract).then_inc(w3_lo, 1)

        @block.scalar
        def _(act):
            act.wait_ge(ids_in, 48)
            act.wait_ge(consts, 1)
            for b in range(1, CB, 2):
                k = act.value_load(ids[0:1, 0, b:b + 1], min_val=0, max_val=NCOND - 1)
                act.dma_start(wbd[C:P, b // 2, C:P],
                              w0[bass.ds(k, 1)].rearrange("o c d -> c (o d)")).then_inc(w0_first_in[1], 16)
            wa = 2 * KB * RANK
            for b in range(HB, CB):
                k = act.value_load(ids[0:1, 1, b:b + 1], min_val=0, max_val=NLORA - 1)
                act.dma_start(agu_of[0, :, b * wa:(b + 1) * wa], agu[k]).then_inc(agu_in[1], 16)

            def fn(dst, src, f, scale=1.0):
                act.activation(dst, src, f, scale=scale).then_inc(ka, 1)

            def sine_u():
                act.wait_ge(par_in, 11 * 16)
                act.wait_ge(kg, KG_U)
                fn(uu[:, :, :], uu[:, :, :], ACT.Sin, TWO_PI)

            def sine_u_quarter():
                fn(ux[:, :, :], ux[:, :, :], ACT.Sin, TWO_PI)

            def sines_of_step():
                act.wait_ge(kg, KG_TH)
                fn(s["s1"][:, :], s["w1"][:, :], ACT.Sin, TWO_PI)
                fn(s["c1"][:, :], s["wc"][:, :], ACT.Sin, TWO_PI)
                fn(s["sh"][:, :], s["w1"][:, :], ACT.Sin, TWO_PI / 2)

            def sine_v():
                act.wait_ge(kg, KG_V)
                fn(vv[:, :, :], vv[:, :, :], ACT.Sin, TWO_PI)

            def exp_u():
                act.wait_ge(kg, KG_UE)
                fn(ue[:, :, :], ue[:, :, :], ACT.Exp)

            def exp_v():
                act.wait_ge(kg, KG_VE)
                fn(ve[:, :, :], ve[:, :, :], ACT.Exp)
                fn(s["th"][:, :], s["adt"][:, :], ACT.Tanh, 0.5)

            def hi(c, u):
                i = u % 2
                n = nth(c, u)
                act.wait_ge(raw_in[i], n * 48)
                act.wait_ge(unit_done[i], n)
                *first, (r, w_hi, _) = split_views(u)
                for r0, w0_hi, _ in first:
                    act.activation(w0_hi, r0, ACT.Copy).then_inc(hi_first, 1)
                act.activation(w_hi, r, ACT.Copy).then_inc(hi_done[i], 1)

            act.activation(silu[0:1, 0:1], ids[0:1, 0, 0:1].bitcast(F32), ACT.Silu).then_inc(silu_table, 1)
            act.wait_ge(silu_table, 1)
            def chunk(c, first, last):
                act.wait_ge(x1_ready, c * KB + CREDIT_X1)
                for q in range(CP):
                    act.wait_ge(l0_done, c * CP + q + 1)
                    b = L0_BANKS[q]
                    act.activation(xhi[:, :, q * P:(q + 1) * P],
                                   ps[:, b:b + 2, :].rearrange("p b (k m) -> p (b k) m", m=P),
                                   ACT.Copy).then_inc(l0_hi, 1)
                    if first and q == 1:
                        hi(c, 0)
                hi(c, 1)
                if not first:
                    act.dma_start(x1_dram[bass.ds(c - 1, 1), :, KB - 1, :].rearrange("o p t -> (o p) t"),
                                  x1out[:, 1, :]).then_inc(x1_stored[1], 16)

                def width_block(f, after_gate=None, after_up=None):
                    for g, more in ((0, after_gate), (1, after_up)):
                        act.wait_ge(raw_in[g], (nth(c, 2) + f) * 48)
                        act.wait_ge(unit_done[g], nth(c, 2) + f)
                        act.activation(whi[:, g, 0:KB + 2, :], raw[:, g, 0:KB + 2, :],
                                       ACT.Copy).then_inc(hi_done[g], 1)
                        if more is not None:
                            more()
                    act.wait_ge(unit_done[0], nth(c, 2) + f + 1)
                    act.wait_ge(mul_done, c * FB + f + 1)
                    act.activation(silu[:, :], ps[:, GATE, :], ACT.Silu).then_inc(silu_done, 1)

                if first:
                    with act.Fori(0, 4) as f:
                        width_block(f)
                    width_block(4, sine_u, sine_u_quarter)
                    width_block(5, sines_of_step, sine_v)
                    width_block(6, exp_u, exp_v)
                with act.Fori(7 if first else 0, FULL) as f:
                    width_block(f)
                for u in (AD0_U, REST_U, AD1_U, DOWN0A_U):
                    hi(c, u)
                act.wait_ge(unit_done[1], nth(c, REST_U) + 1)
                act.wait_ge(mul_done, c * FB + FULL + 1)
                act.activation(silu[0:REST, :], ps[0:REST, GATE, :], ACT.Silu).then_inc(silu_done, 1)
                hi(c, AD2_U)
                hi(c, DOWN0B_U)

                def store(lb, par):
                    if last:
                        return
                    act.wait_ge(x1_ready, c * KB + lb + (1 + CREDIT_X1))
                    act.dma_start(x1_dram[c, :, lb, :], x1out[:, par, :]).then_inc(x1_stored[par], 16)

                with act.Fori(0, KB // 2 - 1) as h:
                    for par in range(2):
                        for i in range(2):
                            n = nth(c, DOWN1_U) + h * 2 + par
                            act.wait_ge(raw_in[i], n * 48)
                            act.wait_ge(unit_done[i], n)
                            act.activation(whi[:, i, :, :], raw[:, i, :, :], ACT.Copy).then_inc(hi_done[i], 1)
                        store(h * 2 + par, par)
                hi(c, UNITS - 2)
                hi(c, UNITS - 1)
                store(KB - 2, 0)
                if not last:
                    hi(c + 1, 0)

            chunk(0, True, False)
            with act.Fori(1, NCH - 1) as c:
                chunk(c, False, False)
            chunk(NCH - 1, False, True)

            act.wait_ge(unit_done[1], 1 + NCH * US)
            with act.Fori(0, C // TRING) as g:
                for j in range(TRING):
                    act.wait_ge(toep_in[j], g * 16 + 16)
                    act.wait_ge(conv_done, g * TRING + (j + 1))
                    act.activation(toep_h[:, j, :], rtoep[:, j, T - 1:T - 1 - TS:-1],
                                   ACT.Copy).then_inc(toep_hi, 1)
                    act.activation(toep[:, j, TS:T], rtoep[:, j, T - 1 - TS::-1],
                                   ACT.Copy).then_inc(toep_ready, 1)
                    act.wait_ge(ug_ready, g * TRING + (j + 1))
                    act.activation(u_hl[:, j, 0, :], ug[:, j, :, :].rearrange("p l b -> p (l b)"),
                                   ACT.Copy).then_inc(u_hi, 1)

            act.wait_ge(w3_ready, 1)
            act.activation(w3hi[:, :, :], wbd[:, :, :], ACT.Copy).then_inc(w3_hi, 1)

            def x2_hi_part(n):
                for k in range(2):
                    act.wait_ge(turned, 2 * n + k + 1)
                    if n >= 2:
                        act.wait_ge(l3_done, 2 * n - 3 + k)
                    act.activation(x2hi[:, n % 2, k * 512:(k + 1) * 512], ps[:, 2 * (n % 2) + k, :],
                                   ACT.Copy).then_inc(x2_hi, 1)

            x2_hi_part(0)
            x2_hi_part(1)
            for n in range(PAIRS):
                act.wait_ge(l3_done, 2 * n + 2)
                if n >= 2:
                    act.wait_ge(out_stored[n % 2], 16 * (n // 2))
                act.activation(ostage[:, n % 2, T // 2:T], ps[:, 5 + 2 * (n % 2), :], ACT.Identity,
                               bias=bcol[:, n:n + 1]).then_inc(out_ready[1], 1)
                if n + 2 < PAIRS:
                    x2_hi_part(n + 2)

        @block.tensor
        def _(pe):
            def products(bank, w, nblk, r_hi, r_lo, start, stop, first=0):
                for k in range(first, first + nblk):
                    for n, (wt, r) in enumerate(((whi, r_hi), (whi, r_lo), (wlo, r_hi))):
                        ins = pe.matmul(bank, wt[:, w, k, :], r(k), start=start and k == first and n == 0,
                                        stop=stop and k == first + nblk - 1 and n == 2)
                return ins

            def s4d_kernel():
                pe.wait_ge(kg, KG_UV)
                per_bank = 512 // LS
                for h in range(C):
                    hb = h % per_bank
                    ins = pe.matmul(ps[0:LS, 4 + h // per_bank, hb * LS:(hb + 1) * LS], uu[:, h, :],
                                    vv[:, h, :], start=True, stop=True)
                ins.then_inc(kp, 1)

            def chunk(c, first):
                pe.wait_ge(w0_ready[0 if first else 1], 1)
                for q in range(CP):
                    pe.wait_ge(x_in[q], c * 16 + 16)
                    if q == 3:
                        pe.wait_ge(l0_lo, c * CP + 1)
                    b = L0_BANKS[q]
                    for k in range(KB):
                        ins = pe.matmul(ps[:, b + k // 4, (k % 4) * P:(k % 4) * P + P],
                                        xn[:, q, k * P:(k + 1) * P],
                                        wbd[:, bass.ds(c * CP + q, 1), :].rearrange("p o d -> p (o d)"),
                                        start=True, stop=True)
                    ins.then_inc(l0_done, 1)
                pe.wait_ge(x1_ready, c * KB + CREDIT_X1)
                for u in range(2):
                    pe.wait_ge(l0_lo, c * CP + 2 * u + 2)
                    pe.wait_ge(lo_done[u], nth(c, u) + 1)
                    t0 = u * TOK // 2
                    products(ps[:, DOWN + u, 0:TOK // 2], u, KB, lambda k: xhi[:, k, t0:t0 + TOK // 2],
                             lambda k: xlo[:, k, t0:t0 + TOK // 2], True, True).then_inc(unit_done[u], 1)

                def x_hi(k):
                    return xhi[:, k, :]

                def x_lo(k):
                    return xlo[:, k, :]

                def lora_b(bank, w, k, g, stop=True):
                    for half in range(2):
                        for n, wt in enumerate((whi, wlo)):
                            last = stop and half == 1 and n == 1
                            ins = pe.matmul(bank[:, half * HT:half * HT + HT], wt[:, w, k + half, :],
                                            t_hl[:, g, half, :], start=False, stop=last)
                    return ins


                def width_block(f):
                    pe.wait_ge(silu_done, c * FB + f + 1)
                    pe.wait_ge(lo_done[0], nth(c, 2) + f + 1)
                    products(ps[:, GATE, :], 0, KB, x_hi, x_lo, True, False)
                    pe.wait_ge(t_ready, c * 5 + 5)
                    lora_b(ps[:, GATE, :], 0, KB, 0).then_inc(unit_done[0], 1)
                    pe.wait_ge(mul_done, c * FB + f + 1)
                    pe.wait_ge(lo_done[1], nth(c, 2) + f + 1)
                    products(ps[:, UP, :], 1, KB, x_hi, x_lo, True, False)
                    lora_b(ps[:, UP, :], 1, KB, 1).then_inc(unit_done[1], 1)

                if first:
                    with pe.Fori(0, TAIL) as f:
                        width_block(f)
                    s4d_kernel()
                with pe.Fori(TAIL if first else 0, FULL) as f:
                    width_block(f)

                def a_down(u):
                    k0, k1 = AD_UNITS[u]
                    pe.wait_ge(act_done, c * FB + k1 + 1)
                    pe.wait_ge(lo_done[u % 2], nth(c, u) + 1)
                    for k in range(k0, k1):
                        for half in range(2):
                            w = (whi, wlo)[half][:, u % 2, k - k0, :]
                            cols = slice(half * HT, half * HT + HT)
                            ins = pe.matmul(ps[:, TDB + half, 0:HT], w, act_hi[:, k, cols], start=k == 0,
                                            stop=k == FULL)
                            if k < FULL:
                                ins = pe.matmul(ps[0:P // 2, TDB + half, 0:HT], w[:, 0:P // 2],
                                                act_lo[:, k, cols], start=False, stop=False)
                    ins.then_inc(unit_done[u % 2], 1)

                def rests():
                    i = REST_U % 2
                    pe.wait_ge(silu_done, c * FB + FULL + 1)
                    pe.wait_ge(lo_done[i], nth(c, REST_U) + 1)
                    products(ps[:, GATE, :], i, KB, x_hi, x_lo, True, False)
                    lora_b(ps[:, GATE, :], i, KB, 0, stop=False)
                    lora_b(ps[:, GATE, :], i, KB + 2, 1).then_inc(unit_done[i], 1)

                def down_a(i, par, lb, n):
                    pe.wait_ge(x1_ready, c * KB + lb + (CREDIT_X1 - 1))
                    pe.wait_ge(lo_done[i], n)
                    products(ps[:, DOWN + par, :], i, D0, lambda k: act_hi[:, k, :], lambda k: act_lo[:, k, :],
                             True, False).then_inc(unit_done[i], 1)

                def down_b(i, par, n):
                    bank = ps[:, DOWN + par, :]
                    pe.wait_ge(lo_done[i], n)
                    products(bank, i, FULL - D0, lambda k: act_hi[:, D0 + k, :],
                             lambda k: act_lo[:, D0 + k, :], False, False)
                    for wt in (whi, wlo):
                        pe.matmul(bank, wt[:, i, FULL - D0, :], act_hi[:, FULL, :], start=False, stop=False)
                    pe.wait_ge(t_ready, c * 5 + 6)
                    lora_b(bank, i, FB - D0, 0).then_inc(unit_done[i], 1)

                a_down(AD0_U)
                rests()
                a_down(AD1_U)
                down_a(DOWN0A_U % 2, 0, 0, nth(c, DOWN0A_U) + 1)
                a_down(AD2_U)
                down_b(DOWN0B_U % 2, 0, nth(c, DOWN0B_U) + 1)

                def down(lb, par):
                    down_a(0, par, lb, nth(c, DOWN1_U) + lb)
                    down_b(1, par, nth(c, DOWN1_U) + lb)

                with pe.Fori(0, KB // 2 - 1) as h:
                    down(h * 2 + 1, 1)
                    down(h * 2 + 2, 0)
                down(KB - 1, 1)

            chunk(0, True)
            with pe.Fori(1, NCH) as c:
                chunk(c, False)

            with pe.Fori(0, C // TRING) as g:
                for j in range(TRING):
                    h = g * TRING + j
                    pe.wait_ge(toep_ready, h + (1 + TRING))
                    pe.wait_ge(toep_lo, h + (1 + TRING))
                    pe.wait_ge(u_lo, h + 1)
                    pe.wait_ge(y_done, h + (1 + CREDIT_Y - 2))
                    y = ps[:, j % 2, 0:KB * B]
                    u = ug[:, j % URING, :, :].rearrange("p l b -> p (l b)")
                    for d in range(KB):
                        block, n = slice(d * P, (d + 1) * P), (KB - d) * B
                        if d < SPLIT:
                            products_of_block = ((toep_h, 0), (toep_h, 1), (toep_l, 0))
                            for m, (tile, part) in enumerate(products_of_block):
                                pe.matmul(y[:, d * B:], tile[:, j, block], u_hl[:, j, part, 0:n],
                                          start=d == 0 and m == 0, stop=False)
                        else:
                            ins = pe.matmul(y[:, d * B:], toep[:, j, block], u[:, 0:n], start=False,
                                            stop=d == KB - 1)
                    ins.then_inc(conv_done, 1)

            pe.wait_ge(x2_done, C + CREDIT_Y)
            pe.wait_ge(w3_ready, 1)

            def turn(n):
                for half in range(2):
                    if n >= 2:
                        pe.wait_ge(x2_lo, 2 * n - 3 + half)
                    for k in range(KB // 2):
                        ins = pe.transpose(ps[:, 2 * (n % 2) + half, k * P:(k + 1) * P],
                                           x1s[:, n // CP, half * (KB // 2) + k, (n % CP) * P:(n % CP) * P + P],
                                           ident[:, :])
                    ins.then_inc(turned, 1)

            turn(0)
            turn(1)
            for n in range(PAIRS):
                if n == 0:
                    pe.wait_ge(w3_lo, 1)
                for k in range(2):
                    pe.wait_ge(x2_lo, 2 * n + k + 1)
                    if n >= 2:
                        pe.wait_ge(out_ready[k], n - 1)
                    for m, (w, x2) in enumerate(((w3hi, x2hi), (w3hi, x2lo), (w3lo, x2hi))):
                        ins = pe.matmul(ps[:, 4 + 2 * (n % 2) + k, :], w[:, n, :],
                                        x2[:, n % 2, k * 512:(k + 1) * 512], start=m == 0, stop=m == 2)
                    ins.then_inc(l3_done, 1)
                if n + 2 < PAIRS:
                    turn(n + 2)

        @block.vector
        def _(dve):
            for i in range(2):
                dve.sem_inc(lo_done[i], 1)
                dve.sem_inc(unit_done[i], 1)
                dve.sem_inc(x1_stored[i], 16)
            dve.sem_inc(silu_done, 1)
            dve.sem_inc(mul_done, 1)
            dve.sem_inc(act_done, 1)
            dve.sem_inc(t_ready, 1)
            dve.sem_inc(x2_done, CREDIT_Y)
            dve.sem_inc(x1_ready, CREDIT_X1)
            dve.sem_inc(conv_done, CREDIT_CONV)
            dve.sem_inc(toep_ready, TRING)
            dve.sem_inc(toep_lo, TRING)
            dve.sem_inc(y_done, CREDIT_Y)

            step = [0]

            def did(ins):
                ins.then_inc(kg, 1)
                step[0] += 1

            def after(n=None):
                dve.wait_ge(kg, step[0] if n is None else n)

            def per_h(t):
                return t[:, :].unsqueeze(2).to_broadcast([P, C, LS])

            powers = jj[:, :].unsqueeze(1).to_broadcast([P, C, LS])
            tt, ts, stt = dve.tensor_tensor, dve.tensor_scalar, dve.scalar_tensor_tensor

            def a(n):
                return s[n][:, :]

            dve.wait_ge(consts, CONSTS_WBD)
            for g in range(2):
                dve.wait_ge(w0_first_in[g], 16 * CP)
            tt(wbd[:, 0:CP, :], wbd[:, 0:CP, :], ident[:, :].unsqueeze(1).to_broadcast([P, CP, P]),
               ALU.add).then_inc(w0_ready[0], 1)

            def step_exponents_and_angles():
                dve.wait_ge(par_in, 11 * 16)
                xe, ke, re_, pe_, te = (t[:, :, :] for t in (ex_x, ex_k, ex_r, ex_p, ex_t))
                did(ts(ke, xe, float(1 / np.log(2)), None, ALU.mult))
                after()
                did(ts(te, ke, ROUND, -ROUND, ALU.add, ALU.add))
                after()
                did(ts(ke, te, -126.0, 127.0, ALU.max, ALU.min))
                after()
                did(stt(re_, ke, -LN2_HI, xe, ALU.mult, ALU.add))
                after()
                did(stt(re_, ke, -LN2_LO, re_, ALU.mult, ALU.add))
                did(ts(te, ke, 127.0, 2.0 ** 23, ALU.add, ALU.mult))
                after()
                did(dve.tensor_copy(ex_i[:, :, :], te))
                did(ts(pe_, re_, 1 / 5040, None, ALU.mult))
                for k in (720, 120, 24, 6, 2, 1):
                    after()
                    did(stt(pe_, pe_, 1 / k, re_, ALU.add, ALU.mult))
                after()
                did(stt(ex_x[:, :, :], pe_, 1.0, ex_i[:, :, :].bitcast(F32), ALU.add, ALU.mult))
                after()
                did(stt(a("adt"), a("ea"), -1.0, a("dt_"), ALU.mult, ALU.mult))
                did(stt(a("w1"), a("aim"), 1 / (2 * np.pi), a("dt_"), ALU.mult, ALU.mult))
                after()
                did(ts(a("tmp"), a("w1"), ROUND, -ROUND, ALU.add, ALU.add))
                did(ts(a("adt32"), a("adt"), float(LS), None, ALU.mult))
                after()
                did(tt(a("w1"), a("w1"), a("tmp"), ALU.subtract))
                after()
                did(ts(a("wc"), a("w1"), 0.25, None, ALU.add))
                after()
                did(ts(a("em"), a("wc"), ROUND, -ROUND, ALU.add, ALU.add))
                after()
                did(tt(a("wc"), a("wc"), a("em"), ALU.subtract))
                assert step[0] == KG_TH, step
                did(ts(a("w2"), a("w1"), float(LS), None, ALU.mult))
                after()
                did(ts(a("tmp"), a("w2"), ROUND, -ROUND, ALU.add, ALU.add))
                after()
                did(tt(a("w2"), a("w2"), a("tmp"), ALU.subtract))
                after()

            def u_angles():
                did(tt(uu[:, :, :], per_h(s["w2"]), powers, ALU.mult))
                after()
                did(ts(ux[:, :, :], uu[:, :, :], 0.25, None, ALU.add))
                did(ts(ve[:, :, :], uu[:, :, :], ROUND, -ROUND, ALU.add, ALU.add))
                after()

            def u_angles_to_turns():
                did(tt(uu[:, :, :], uu[:, :, :], ve[:, :, :], ALU.subtract))
                after()
                did(ts(ve[:, :, :], ux[:, :, :], ROUND, -ROUND, ALU.add, ALU.add))
                after()
                did(tt(ux[:, :, :], ux[:, :, :], ve[:, :, :], ALU.subtract))
                assert step[0] == KG_U, step
                after()

            def v_angles():
                did(tt(vv[:, :, :], per_h(s["w1"]), powers, ALU.mult))
                after()
                did(ts(vv[:, :, :], vv[:, :, :], ph[:, 0:1], None, ALU.add))
                after()
                did(ts(ve[:, :, :], vv[:, :, :], ROUND, -ROUND, ALU.add, ALU.add))
                after()

            def v_angles_to_turns_and_u_exponents():
                did(tt(vv[:, :, :], vv[:, :, :], ve[:, :, :], ALU.subtract))
                assert step[0] == KG_V, step
                after()
                did(tt(ue[:, :, :], per_h(s["adt32"]), powers, ALU.mult))
                assert step[0] == KG_UE, step

            def v_exponents():
                did(tt(ve[:, :, :], per_h(s["adt"]), powers, ALU.mult))
                assert step[0] == KG_VE, step

            def coefficients():
                dve.wait_ge(ka, KA_ALL)
                after()
                did(ts(a("tmp"), a("th"), -1.0, 1.0, ALU.mult, ALU.add))
                did(tt(a("sh"), a("sh"), a("sh"), ALU.mult))
                did(tt(a("n2"), a("ea"), a("ea"), ALU.mult))
                did(tt(a("cr"), a("aim"), a("aim"), ALU.mult))
                after()
                did(dve.reciprocal(a("tmp"), a("tmp")))
                did(tt(a("n2"), a("n2"), a("cr"), ALU.add))
                after()
                did(stt(a("em"), a("th"), 2.0, a("tmp"), ALU.mult, ALU.mult))
                did(dve.reciprocal(a("n2"), a("n2")))
                after()
                did(tt(a("er"), a("em"), a("c1"), ALU.mult))
                did(stt(a("ei"), a("em"), 1.0, a("s1"), ALU.add, ALU.mult))
                after()
                did(stt(a("er"), a("sh"), -2.0, a("er"), ALU.mult, ALU.add))
                after()
                did(tt(a("qr"), a("ei"), a("aim"), ALU.mult))
                did(tt(a("tmp"), a("er"), a("ea"), ALU.mult))
                did(tt(a("qi"), a("ei"), a("ea"), ALU.mult))
                did(tt(a("cr"), a("er"), a("aim"), ALU.mult))
                after()
                did(tt(a("qr"), a("qr"), a("tmp"), ALU.subtract))
                did(tt(a("qi"), a("qi"), a("cr"), ALU.add))
                after()
                did(tt(a("qr"), a("qr"), a("n2"), ALU.mult))
                did(stt(a("qi"), a("qi"), -1.0, a("n2"), ALU.mult, ALU.mult))
                after()
                did(tt(a("cr"), a("cre"), a("qr"), ALU.mult))
                did(tt(a("tmp"), a("cim"), a("qi"), ALU.mult))
                did(tt(a("ci"), a("cre"), a("qi"), ALU.mult))
                did(tt(a("er"), a("cim"), a("qr"), ALU.mult))
                after()
                did(tt(a("cr"), a("cr"), a("tmp"), ALU.subtract))
                did(tt(a("ci"), a("ci"), a("er"), ALU.add))
                after()
                did(ts(s["al"][0:C, :], s["cr"][0:C, :], 2.0, None, ALU.mult))
                did(ts(s["al"][C:P, :], s["ci"][C:P, :], -2.0, None, ALU.mult))
                did(ts(s["be"][0:C, :], s["ci"][0:C, :], -2.0, None, ALU.mult))
                did(ts(s["be"][C:P, :], s["cr"][C:P, :], -2.0, None, ALU.mult))
                after()

            def magnitudes_of_v_and_u():
                did(tt(vv[:, :, :], vv[:, :, :], ve[:, :, :], ALU.mult))
                did(tt(uu[:, :, :], uu[:, :, :], ue[:, :, :], ALU.mult))
                after()

            def u_times_c():
                did(tt(ux[:, :, :], ux[:, :, :], ue[:, :, :], ALU.mult))
                did(tt(uu[:, :, :], uu[:, :, :], per_h(s["be"]), ALU.mult))
                after()

            def sum_of_u():
                did(tt(ux[:, :, :], ux[:, :, :], per_h(s["al"]), ALU.mult))
                after()
                did(tt(uu[:, :, :], uu[:, :, :], ux[:, :, :], ALU.add))
                assert step[0] == KG_UV, step

            def kernel_rows():
                dve.wait_ge(kp, 1)
                did(dve.tensor_copy(ksb[:, :, :].rearrange("p h j -> p (h j)"),
                                    ps[0:LS, 4:8, :].rearrange("p a b -> p (a b)")))
                after()
                did(stt(ksb[:, :, LS - 1], dd[:, :], e_last[:, 0:1], ksb[:, :, LS - 1], ALU.mult, ALU.add))
                assert step[0] == KG_K, step
                after()

            def f32(t):
                return t.bitcast(F32)

            def lo(c, u):
                i = u % 2
                *first, (r, w_hi, w_lo) = split_views(u)
                for r0, w0_hi, w0_lo in first:
                    dve.wait_ge(hi_first, first_pieces(c, u))
                    tt(w0_lo, r0, f32(w0_hi), ALU.subtract)
                dve.wait_ge(hi_done[i], nth(c, u))
                tt(w_lo, r, f32(w_hi), ALU.subtract).then_inc(lo_done[i], 1)

            TSC = 10

            def lora_t_gate_up(c, u):
                n = c * TSC + 3 * u
                dve.wait_ge(t_ready, c * 5 + 1)
                cols = slice(u * HT, u * HT + HT)
                tt(t32[:, cols].rearrange("p (b n) -> p b n", n=C),
                   ps[:, DOWN + u, 0:HT].rearrange("p (b n) -> p b n", n=C),
                   mask4[:, :].unsqueeze(2).to_broadcast([P, HB, C]), ALU.mult).then_inc(t_step, 1)
                dve.wait_ge(t_step, n + 1)
                for g in range(2):
                    mine = slice(64 * g, 64 * g + 64)
                    dve.tensor_copy(t_hl[mine, g, u, :], t32[mine, cols]).then_inc(t_step, 1)
                for g in range(2):
                    mine, other = slice(64 * g, 64 * g + 64), slice(64 - 64 * g, P - 64 * g)
                    dve.wait_ge(t_step, n + 2 + g)
                    tt(t_hl[other, g, u, :], t32[mine, cols], f32(t_hl[mine, g, u, :]),
                       ALU.subtract).then_inc(t_ready, 1)

            def lora_t_down(c):
                n = c * TSC + 6
                top = t32[0:64, :]
                halves = top.rearrange("p (f n) -> p f n", n=HT)
                dve.wait_ge(t_ready, c * 5 + 5)
                dve.tensor_copy(halves, ps[64:P, TDB:TDB + 2, 0:HT]).then_inc(t_step, 1)
                dve.wait_ge(t_step, n + 1)
                tt(halves, halves, ps[0:64, TDB:TDB + 2, 0:HT], ALU.add).then_inc(t_step, 1)
                dve.wait_ge(t_step, n + 2)
                by_batch = top.rearrange("p (f b n) -> p f b n", f=2, n=C)
                tt(by_batch, by_batch, mask4[0:64, :].unsqueeze(1).unsqueeze(3).to_broadcast([64, 2, HB, C]),
                   ALU.mult).then_inc(t_step, 1)
                dve.wait_ge(t_step, n + 3)
                dve.tensor_copy(t_hl[0:64, 0, :, :], halves).then_inc(t_step, 1)
                dve.wait_ge(t_step, n + 4)
                tt(t_hl[64:P, 0, :, :], halves, f32(t_hl[0:64, 0, :, :]), ALU.subtract).then_inc(t_ready, 1)

            full = slice(0, P)

            def gate_up(c, f, rows, up):
                n = c * FB + f
                dve.wait_ge(silu_done, n + 2)
                dve.wait_ge(act_done, n + 1)
                tt(act32[rows, :], silu[rows, :], up, ALU.mult).then_inc(mul_done, 1)
                dve.wait_ge(mul_done, n + 2)
                if rows == full:
                    a_hi, a_lo = (t[:, bass.ds(f, 1), :].rearrange("p o t -> p (o t)")
                                  for t in (act_hi, act_lo))
                else:
                    a_hi, a_lo = act_hi[rows, FULL, :], act_hi[REST:P, FULL, :]
                dve.tensor_copy(a_hi, act32[rows, :]).then_inc(act_hi_done, 1)
                dve.wait_ge(act_hi_done, n + 1)
                tt(a_lo, act32[rows, :], f32(a_hi), ALU.subtract).then_inc(act_done, 1)

            def residual(c, lb, par, last):
                dve.wait_ge(unit_done[1], nth(c, DOWN0B_U) + lb + 1)
                if last:
                    dve.wait_ge(res_step, c * KB + lb + 1)
                    o = x1s[:, NCH - 1, bass.ds(lb, 1), :].rearrange("p o t -> p (o t)")
                    tt(o, ps[:, DOWN + par, :], o, ALU.add).then_inc(x1_ready, 1)
                    return
                dve.wait_ge(x1_stored[par], c * (KB // 2 * 16) + (lb - par) * 8 + 16)
                o = x1out[:, par, :]
                tt(o, ps[:, DOWN + par, :], f32(xhi[:, bass.ds(lb, 1), :]).rearrange("p o t -> p (o t)"),
                   ALU.add).then_inc(res_step, 1)
                dve.wait_ge(res_step, c * KB + lb + 1)
                tt(o, o, f32(xlo[:, bass.ds(lb, 1), :]).rearrange("p o t -> p (o t)"),
                   ALU.add).then_inc(x1_ready, 1)

            def fold_x0(lb):
                tt(x1s[:, NCH - 1, bass.ds(lb, 1), :], f32(xhi[:, bass.ds(lb, 1), :]),
                   f32(xlo[:, bass.ds(lb, 1), :]), ALU.add).then_inc(res_step, 1)

            def chunk(c, first, last):
                for q in range(CP):
                    dve.wait_ge(l0_hi, c * CP + q + 1)
                    b = L0_BANKS[q]
                    sl = slice(q * P, (q + 1) * P)
                    tt(xlo[:, :, sl], ps[:, b:b + 2, :].rearrange("p b (k m) -> p (b k) m", m=P),
                       f32(xhi[:, :, sl]), ALU.subtract).then_inc(l0_lo, 1)
                    if first and q == 1:
                        lo(c, 0)
                lo(c, 1)
                if first:
                    dve.wait_ge(consts, CONSTS)
                lo(c, 2)
                for u in range(2):
                    dve.wait_ge(unit_done[u], nth(c, u) + 1)
                    lora_t_gate_up(c, u)
                lo(c, 3)
                if first:
                    step_exponents_and_angles()

                def width_block(f):
                    for g in range(2):
                        dve.wait_ge(hi_done[g], nth(c, 2) + f)
                        tt(wlo[:, g, 0:KB + 2, :], raw[:, g, 0:KB + 2, :], f32(whi[:, g, 0:KB + 2, :]),
                           ALU.subtract).then_inc(lo_done[g], 1)
                        if g == 0:
                            dve.wait_ge(unit_done[1], nth(c, 2) + f)
                            gate_up(c, f - 1, full, ps[:, UP, :])

                if first:
                    pieces = (u_angles, u_angles_to_turns, v_angles, v_angles_to_turns_and_u_exponents,
                              v_exponents, None, coefficients, magnitudes_of_v_and_u, u_times_c, sum_of_u,
                              kernel_rows)
                    assert len(pieces) == TAIL
                    for f, piece in enumerate(pieces, 1):
                        width_block(f)
                        if piece is not None:
                            piece()
                with dve.Fori(TAIL + 1 if first else 1, FULL) as f:
                    width_block(f)
                lo(c, AD0_U)
                dve.wait_ge(unit_done[1], nth(c, REST_U - 2) + 1)
                gate_up(c, FULL - 1, full, ps[:, UP, :])
                lo(c, REST_U)
                lo(c, AD1_U)
                lo(c, DOWN0A_U)
                gate_up(c, FULL, slice(0, REST), ps[REST:P, GATE, :])
                lo(c, AD2_U)
                lo(c, DOWN0B_U)
                dve.wait_ge(unit_done[0], nth(c, AD2_U) + 1)
                lora_t_down(c)
                if first:
                    dve.wait_ge(k_stored, 32)
                if last:
                    fold_x0(0)
                with dve.Fori(0, KB // 2 - 1) as h:
                    for par in range(2):
                        lb = h * 2 + par
                        for i in range(2):
                            dve.wait_ge(hi_done[i], nth(c, DOWN1_U) + lb)
                            tt(wlo[:, i, :, :], raw[:, i, :, :], f32(whi[:, i, :, :]),
                               ALU.subtract).then_inc(lo_done[i], 1)
                            if i == 0:
                                residual(c, lb, par, last)
                                if last:
                                    fold_x0(lb + 1)
                lo(c, UNITS - 2)
                residual(c, KB - 2, 0, last)
                if last:
                    fold_x0(KB - 1)
                lo(c, UNITS - 1)
                if not last:
                    lo(c + 1, 0)
                residual(c, KB - 1, 1, last)

            chunk(0, True, False)
            with dve.Fori(1, NCH - 1) as c:
                chunk(c, False, False)
            dve.tensor_copy(len_f[:, :], len_i[:, :]).then_inc(mask_ready, 1)
            dve.wait_ge(mask_ready, 2)
            tt(mask[:, :, :], mask[:, :, :], len_f[:, :].unsqueeze(1).to_broadcast([P, KB, B]),
               ALU.is_lt).then_inc(mask_ready, 1)
            chunk(NCH - 1, False, True)

            dve.wait_ge(mask_ready, 3)
            dve.wait_ge(x1_in, 16 * 5)
            x1h = x1s[:, :, :, :].rearrange("p c l (b h) -> p l c b h", h=C)

            def conv_lo(h, j):
                dve.wait_ge(toep_hi, h + 1)
                tt(toep_l[:, j, :], rtoep[:, j, T - 1:T - 1 - TS:-1], f32(toep_h[:, j, :]),
                   ALU.subtract).then_inc(toep_lo, 1)
                dve.wait_ge(u_hi, h + 1)
                tt(u_hl[:, j, 1, :], ug[:, j, :, :].rearrange("p l b -> p (l b)"), f32(u_hl[:, j, 0, :]),
                   ALU.subtract).then_inc(u_lo, 1)

            def conv_out(h, j):
                dve.wait_ge(conv_done, h + (1 + CREDIT_CONV))
                dve.wait_ge(x2_done, h + (1 + CREDIT_Y - 2))
                y = yv[:, j % 2, :, :]
                tt(y, ps[:, j % 2, 0:KB * B].rearrange("p (l b) -> p l b", b=B), mask[:, :, :],
                   ALU.mult).then_inc(y_done, 1)
                dve.wait_ge(y_done, h + (1 + CREDIT_Y))
                xh = x1h[:, :, :, :, h]
                tt(xh, xh, y.rearrange("p l (c b) -> p l c b", c=NCH), ALU.add).then_inc(x2_done, 1)

            conv_lo(0, 0)
            conv_lo(1, 1)
            with dve.Fori(0, C // TRING - 1) as g:
                for j in range(TRING):
                    h = g * TRING + j
                    conv_lo(h + 2, (j + 2) % TRING)
                    conv_out(h, j)
            for h in range(C - TRING, C):
                if h + 2 < C:
                    conv_lo(h + 2, (h + 2) % TRING)
                conv_out(h, h % TRING)
            def x2_lo_part(n):
                for k in range(2):
                    dve.wait_ge(x2_hi, 2 * n + k + 1)
                    if n >= 2:
                        dve.wait_ge(l3_done, 2 * n - 3 + k)
                    half = slice(k * 512, (k + 1) * 512)
                    tt(x2lo[:, n % 2, half], ps[:, 2 * (n % 2) + k, :], f32(x2hi[:, n % 2, half]),
                       ALU.subtract).then_inc(x2_lo, 1)

            x2_lo_part(0)
            x2_lo_part(1)
            for n in range(PAIRS):
                dve.wait_ge(l3_done, 2 * n + 1)
                if n >= 2:
                    dve.wait_ge(out_stored[n % 2], 16 * (n // 2))
                ts(ostage[:, n % 2, 0:T // 2], ps[:, 4 + 2 * (n % 2), :], bcol[:, n:n + 1], None,
                   ALU.add).then_inc(out_ready[0], 1)
                if n + 2 < PAIRS:
                    x2_lo_part(n + 2)


def kernel(x, itok_B_0_15, itok_B_2_6, itok_B_78_3631, itok_B_0_31, L0_cond_weights, L1_cond_W_gate,
           L1_cond_W_up, L1_cond_W_down, L1_cond_A_gate, L1_cond_B_gate, L1_cond_A_up, L1_cond_B_up,
           L1_cond_A_down, L1_cond_B_down, L2_cond_log_dt, L2_cond_C, L2_cond_log_A_real, L2_cond_A_imag,
           L2_cond_D, L3_cond_weights, L3_cond_biases):
    import concourse.bacc as bacc
    from concourse.bass_utils import run_bass_kernel_spmd

    n = np.asarray
    cut = FULL * P

    def gate_up_blocks(gate, up, axis_rows):
        g, u = gate[:, :cut].reshape(-1, FULL, P), up[:, :cut].reshape(-1, FULL, P)
        return np.stack([g, u], 2).reshape(-1, 2 * FULL, P)

    wg, wu = n(L1_cond_W_gate).T, n(L1_cond_W_up).T
    w = np.concatenate([gate_up_blocks(wg, wu, T), np.concatenate([wg[:, cut:], wu[:, cut:]], 1)[:, None]], 1)
    wgu = w.reshape(KB, P, GU, P).transpose(2, 1, 0, 3)
    bg = n(L1_cond_B_gate)[0].transpose(0, 2, 1).reshape(NLORA * RANK, F)
    bu = n(L1_cond_B_up)[0].transpose(0, 2, 1).reshape(NLORA * RANK, F)
    zero = np.zeros((NLORA * RANK, REST), np.float32)
    bgu = np.concatenate([gate_up_blocks(bg, bu, 0).reshape(NLORA * RANK, -1), bg[:, cut:], zero, zero,
                          bu[:, cut:]], 1).reshape(NLORA, RANK, GU + 1, P)
    a = np.stack([n(L1_cond_A_gate)[0], n(L1_cond_A_up)[0]], 1)
    agu = a.reshape(NLORA, 2, RANK, KB, P).transpose(0, 4, 1, 3, 2).reshape(NLORA, P, -1)
    ad = n(L1_cond_A_down)[0]
    ad = np.concatenate([ad, ad[:, :, cut:]], 2)
    ad = ad.reshape(NLORA, RANK, FB, P).transpose(0, 3, 2, 1).reshape(NLORA, P, -1)
    wd = n(L1_cond_W_down).T
    wd = np.concatenate([wd, wd[cut:]], 0)
    wd = wd.reshape(FB, P, KB, P).transpose(2, 1, 0, 3)
    bd = n(L1_cond_B_down)[0].transpose(0, 2, 1).reshape(NLORA, RANK, KB, P)
    arrays = {
        "x": n(x).reshape(B * C, T), "cond": n(itok_B_0_15).reshape(1, B), "lora": n(itok_B_2_6).reshape(1, B),
        "length": n(itok_B_78_3631), "subj": n(itok_B_0_31).reshape(1, B),
        "w0": n(L0_cond_weights), "wgu": wgu, "wd": wd, "agu": agu, "ad": ad, "bgu": bgu, "bd": bd,
        "log_dt": n(L2_cond_log_dt), "c_ri": n(L2_cond_C).transpose(2, 1, 0), "log_ar": n(L2_cond_log_A_real).T,
        "a_im": n(L2_cond_A_imag).T, "d_skip": n(L2_cond_D).reshape(1, C),
        "w3": n(L3_cond_weights), "bias": n(L3_cond_biases).reshape(NSUBJ, C),
    }
    nc = bacc.Bacc("TRN2", target_bir_lowering=False, num_devices=1)
    arrays = {f"in_{k}": np.ascontiguousarray(v) for k, v in arrays.items()}
    aps = {k[3:]: nc.dram_tensor(k, v.shape, mybir.dt.from_np(v.dtype), kind="ExternalInput").ap()
           for k, v in arrays.items()}
    out = nc.dram_tensor("out", (B * C, T), F32, kind="ExternalOutput").ap()
    build(nc, out=out, **aps)
    r = run_bass_kernel_spmd(nc, [arrays], core_ids=[0])
    return r.results[0]["out"].reshape(B, C, T)
```
